# Optimizing a Trainium2 kernel written in Bass

```python
import numpy as np
import jax
import jax.numpy as jnp

def _softmax(x, axis=-1):
    return jax.nn.softmax(x, axis=axis)

def _gelu(x):
    return jax.nn.gelu(x, approximate=True)

def _silu(x):
    return jax.nn.silu(x)

def _sigmoid(x):
    return jax.nn.sigmoid(x)

def _layernorm(x, axis=-1, eps=1e-05):
    m = jnp.mean(x, axis=axis, keepdims=True)
    v = jnp.var(x, axis=axis, keepdims=True)
    return (x - m) / jnp.sqrt(v + eps)

def _scatter_add(tgt, idx, src, axis=0):
    return tgt.at[idx].add(src)

def _segment_sum(src, seg, n):
    return jax.ops.segment_sum(src, seg, n)
kernel_name = 'mk_xattn_ffn_d1_seqx_r2_03801f'

def setup_inputs(seed: int=0):
    np.random.seed(seed)
    _w = jnp.asarray

    def _rec_inputs():
        import jax
        import jax.numpy as jnp
        _rk = jax.random.key(seed)
        x = 7.22e-05 + 1 * jax.random.normal(jax.random.fold_in(_rk, 1), (4, 1024, 1024), jnp.float32)
        _lenS = 1024 - jax.random.randint(jax.random.fold_in(_rk, 7), (4,), 0, max(1, 1024 // 4) + 1, jnp.int32)
        _lenS2 = 1024 - jax.random.randint(jax.random.fold_in(_rk, 8), (4,), 0, max(1, 1024 // 4) + 1, jnp.int32)
        _ctx_1024P = jax.random.normal(jax.random.fold_in(_rk, 11), (4, 16, 512), jnp.float32)
        _ctx_1024c = jax.random.dirichlet(jax.random.fold_in(_rk, 511), 0.3 * jnp.ones((16,), jnp.float32), (4, 1024))
        _ctx_1024t = jnp.einsum('bsk,bkd->bsd', _ctx_1024c, _ctx_1024P)
        _ctx_1024t = _ctx_1024t * jax.lax.rsqrt(jnp.mean(jnp.square(_ctx_1024t)) + 1e-12) * 0.953939
        ctx_1024 = 2.81802e-05 + 1.00001 * (_ctx_1024t + 0.3 * jax.random.normal(jax.random.fold_in(_rk, 611), (4, 1024, 512), jnp.float32))
        return (x, ctx_1024)
    x, ctx_1024 = _rec_inputs()

    def _L0_xattn_setup():
        import jax, jax.numpy as jnp
        import numpy as np
        key = jax.random.key(seed)
        ks = jax.random.split(key, 6)
        B, L, N, C, D = (8, 256, 1024, 512, 128)
        return {'teacher_logits': jax.random.normal(ks[0], (B, L, N), dtype=jnp.float32), 'teacher_features': jax.random.normal(ks[1], (B, N, C), dtype=jnp.float32), 'Wq': jax.random.normal(ks[2], (D, C), dtype=jnp.float32) * (1.0 / np.sqrt(C)), 'bq': jnp.zeros((D,), dtype=jnp.float32), 'Wk': jax.random.normal(ks[3], (D, C), dtype=jnp.float32) * (1.0 / np.sqrt(C)), 'bk': jnp.zeros((D,), dtype=jnp.float32)}
    _L0_xattn_all = _L0_xattn_setup()
    _L0_xattn_in = {k: v for k, v in _L0_xattn_all.items() if k in ('Wq', 'bq', 'Wk', 'bk')}
    del _L0_xattn_all

    def _L0_ffn_setup():
        import jax, jax.numpy as jnp
        import numpy as np
        SWIGLU_ALPHA = 1.702
        SWIGLU_LIMIT = 7.0
        B, S, H, E, K, I = (2, 1024, 1024, 32, 4, 512)
        key = jax.random.key(seed)
        ks = jax.random.split(key, 8)
        return {'hidden_states': jax.random.normal(ks[0], (B, S, H), jnp.float32), 'gate_w': jax.random.normal(ks[1], (E, H), jnp.float32) * 0.02, 'gate_b': jnp.zeros((E,), jnp.float32), 'w_gate': jax.random.normal(ks[2], (E, H, I), jnp.float32) * 0.02, 'b_gate': jnp.zeros((E, I), jnp.float32), 'w_up': jax.random.normal(ks[3], (E, H, I), jnp.float32) * 0.02, 'b_up': jnp.zeros((E, I), jnp.float32), 'w_down': jax.random.normal(ks[4], (E, I, H), jnp.float32) * 0.02, 'b_down': jnp.zeros((E, H), jnp.float32)}
    _L0_ffn_all = _L0_ffn_setup()
    _L0_ffn_in = {k: v for k, v in _L0_ffn_all.items() if k in ('gate_w', 'gate_b', 'w_gate', 'b_gate', 'w_up', 'b_up', 'w_down', 'b_down')}
    del _L0_ffn_all
    return {'x': x, 'ctx_1024': ctx_1024, 'L0_xattn_Wq': _L0_xattn_in['Wq'], 'L0_xattn_bq': _L0_xattn_in['bq'], 'L0_xattn_Wk': _L0_xattn_in['Wk'], 'L0_xattn_bk': _L0_xattn_in['bk'], 'L0_ffn_gate_w': _L0_ffn_in['gate_w'], 'L0_ffn_gate_b': _L0_ffn_in['gate_b'], 'L0_ffn_w_gate': _L0_ffn_in['w_gate'], 'L0_ffn_b_gate': _L0_ffn_in['b_gate'], 'L0_ffn_w_up': _L0_ffn_in['w_up'], 'L0_ffn_b_up': _L0_ffn_in['b_up'], 'L0_ffn_w_down': _L0_ffn_in['w_down'], 'L0_ffn_b_down': _L0_ffn_in['b_down']}

def reference(x, ctx_1024, L0_xattn_Wq, L0_xattn_bq, L0_xattn_Wk, L0_xattn_bk, L0_ffn_gate_w, L0_ffn_gate_b, L0_ffn_w_gate, L0_ffn_b_gate, L0_ffn_w_up, L0_ffn_b_up, L0_ffn_w_down, L0_ffn_b_down):
    import jax
    import jax.numpy as jnp

    def _L0_xattn_ref(teacher_logits, teacher_features, Wq, bq, Wk, bk):
        import jax, jax.numpy as jnp
        import numpy as np
        query = jnp.einsum('bnc,dc->bnd', teacher_features, Wq) + bq
        key = jnp.einsum('bnc,dc->bnd', teacher_features, Wk) + bk
        energy = jnp.einsum('bnd,bmd->bnm', query, key)
        attention = jax.nn.softmax(energy, axis=-1)
        x_m = jnp.einsum('bln,bmn->blm', teacher_logits, attention)
        return x_m

    def _L0_ffn_ref(hidden_states, gate_w, gate_b, w_gate, b_gate, w_up, b_up, w_down, b_down):
        import jax, jax.numpy as jnp
        import numpy as np
        SWIGLU_ALPHA = 1.702
        SWIGLU_LIMIT = 7.0
        B, S, H, E, K, I = (2, 1024, 1024, 32, 4, 512)
        Bb, Ss, Hh = hidden_states.shape
        x = hidden_states.reshape(-1, Hh)
        logits = x @ gate_w.T + gate_b
        topk_logits, topk_idx = jax.lax.top_k(logits, K)
        topk_weight = jax.nn.softmax(topk_logits.astype(jnp.float32), axis=-1)
        flat_idx = topk_idx.reshape(-1)
        xs = jnp.repeat(x, K, axis=0)
        order = jnp.argsort(flat_idx)
        xt = xs[order]
        gid = flat_idx[order]
        group_sizes = jnp.bincount(flat_idx, length=E).astype(jnp.int32)
        gate = jax.lax.ragged_dot(xt, w_gate, group_sizes) + b_gate[gid]
        up = jax.lax.ragged_dot(xt, w_up, group_sizes) + b_up[gid]
        gate = jnp.minimum(gate, SWIGLU_LIMIT)
        up = jnp.clip(up, -SWIGLU_LIMIT, SWIGLU_LIMIT)
        glu = gate * jax.nn.sigmoid(SWIGLU_ALPHA * gate)
        activated = (up + 1.0) * glu
        outs = jax.lax.ragged_dot(activated, w_down, group_sizes) + b_down[gid]
        inv = jnp.argsort(order)
        outs = outs[inv].reshape(-1, K, Hh)
        y = jnp.sum(outs * topk_weight[..., None], axis=1).astype(x.dtype)
        return y.reshape(Bb, Ss, Hh)
    x = x + _L0_xattn_ref(_layernorm(x, axis=-1), ctx_1024, L0_xattn_Wq, L0_xattn_bq, L0_xattn_Wk, L0_xattn_bk)
    x = x + _L0_ffn_ref(_layernorm(x, axis=-1), L0_ffn_gate_w, L0_ffn_gate_b, L0_ffn_w_gate, L0_ffn_b_gate, L0_ffn_w_up, L0_ffn_b_up, L0_ffn_w_down, L0_ffn_b_down)
    return x

_drawn_inputs = setup_inputs


def setup_inputs(seed=0):
    import zlib

    import numpy as np

    out = dict(_drawn_inputs(seed))
    spreads = {'L0_xattn_bq': (0.0, 0.1),
     'L0_xattn_bk': (0.0, 0.8),
     'L0_ffn_gate_b': (0.0, 0.1),
     'L0_ffn_b_gate': (0.0, 0.572),
     'L0_ffn_b_up': (0.0, 0.8),
     'L0_ffn_b_down': (0.0, 0.1)}
    factors = {}
    for name, (base, spread) in spreads.items():
        noise = np.random.default_rng([zlib.crc32(name.encode()), seed]).standard_normal(out[name].shape)
        drawn = base * np.exp(spread * noise) if base else spread * noise
        out[name] = jnp.asarray(drawn.astype(out[name].dtype))
    for name, factor in factors.items():
        out[name] = (out[name] * factor).astype(out[name].dtype)
    return out
```

```python
from contextlib import ExitStack

import concourse.bass as bass
from concourse import mybir

ALU = mybir.AluOpType
ACT = mybir.ActivationFunctionType
AX_X = mybir.AxisListType.X
F32 = mybir.dt.float32
F16 = mybir.dt.float16
I32 = mybir.dt.int32
U32 = mybir.dt.uint32

P = 128
EPS = 1e-5
ALPHA = 1.702
LIMIT = 7.0
TOPK = 4
S_ROWS = 256.0
S_PROB = 16384.0
S_W = 256.0
S_ACT = 256.0
CHUNK = 2048
MIN_TILES = 3


class Tally:

    def __init__(self, sem, base=0):
        self.sem, self.base, self.n = sem, base, 0

    def inc(self, instruction, by=1):
        instruction.then_inc(self.sem, by)
        self.n += by

    def now(self):
        return self.base + self.n


def alone(eng, sem, value, passed):
    eng.wait_ge(sem, value)
    eng.sem_inc(passed, 1)


def at(nc, value, most):
    return bass.ds(nc.s_assert_within(value, 0, most, skip_runtime_bounds_check_because="guarded by the loops"), 1)


def xattn_moe_kernel(nc, x, ctx_in, Wq, bq, Wk, bk, gate_w, gate_b, w_gate, b_gate, w_up, b_up,
                     w_down, b_down, acc):
    B, L, H = x.shape
    C = ctx_in.shape[2]
    D = Wq.shape[0]
    E, _, I = w_gate.shape
    T = B * L
    NT = L // P
    KH, KC, KI = H // P, C // P, I // P
    HALF = 512
    assert L == H == 1024 and D == P and acc.shape[0] == T + P
    SLOTS = E * T
    NCHUNK = 3 * KH * I // CHUNK
    MAXT = 256
    assert T * TOPK // P + E * MIN_TILES <= MAXT - 4

    x_rows = x.rearrange("b (t p) h -> b t p h", p=P)
    acc_rows = acc.rearrange("(n p) h -> n p h", p=P)
    xn_tab = nc.dram_tensor("xn_tab", (T + P, 2 * H), F16, kind="Internal").ap()
    xn_rows = xn_tab.rearrange("(n p) h -> n p h", p=P)
    slots = nc.dram_tensor("slots", (SLOTS + 2 * P, 4), I32, kind="Internal").ap()

    with ExitStack() as whole:
        ident16 = whole.enter_context(nc.sbuf_tensor("ident16", [P, P], F16))
        tile_start = whole.enter_context(nc.sbuf_tensor("tile_start", [1, 64], I32))
        slot_row = whole.enter_context(nc.sbuf_tensor("slot_row", [1, MAXT], I32))
        attention_and_routing(nc, locals())
        experts(nc, locals())


def attention_and_routing(nc, g):
    B, L, H, C, D, E, T = g["B"], g["L"], g["H"], g["C"], g["D"], g["E"], g["T"]
    NT, KH, KC, HALF, SLOTS, MAXT = g["NT"], g["KH"], g["KC"], g["HALF"], g["SLOTS"], g["MAXT"]
    x_rows, acc_rows, xn_rows, slots = g["x_rows"], g["acc_rows"], g["xn_rows"], g["slots"]
    ident16, tile_start, slot_row = g["ident16"], g["tile_start"], g["slot_row"]
    ctx_in, acc, xn_tab = g["ctx_in"], g["acc"], g["xn_tab"]

    with ExitStack() as ctx:
        def sb(name, shape, dt):
            return ctx.enter_context(nc.sbuf_tensor(name, shape, dt))

        def psum(name, shape, dt):
            return ctx.enter_context(nc.psum_tensor(name, shape, dt))

        def sem(name):
            return ctx.enter_context(nc.semaphore(name))

        xr = sb("xr", [P, NT, H], F32)
        cx = sb("cx", [P, NT, C], F32)
        cxT = sb("cxT", [P, KC, L], F32)
        qk = sb("qk", [P, 2, L], F32)
        XT = sb("XT", [P, 2, KH, L], F16)
        AT = sb("AT", [P, 2, KH, L], F16)
        xs = sb("xs", [P, H], F32)
        xnh = sb("xnh", [P, 2, H], F16)
        prob = sb("prob", [P, 2, L], F32)
        ah = sb("ah", [P, 2, 2, L], F16)
        xs2 = sb("xs2", [P, 2, H], F32)
        x2h = sb("x2h", [P, 2, 2, H], F16)
        x2T = sb("x2T", [P, KH, P], F32)
        ident = sb("ident", [P, P], F32)
        before = sb("before", [P, P], F32)
        upto = sb("upto", [E, E], F32)
        ones = sb("ones", [P, P], F32)
        WT = sb("WT", [P, 2, KC, D], F32)
        gateT = sb("gateT", [P, KH, E], F32)
        bqk = sb("bqk", [P, 2], F32)
        gb = sb("gb", [P, E], F32)
        iota_i = sb("iota_i", [P, E], I32)
        iota_e = sb("iota_e", [P, E], F32)
        ebase = sb("ebase", [P, E], F32)
        tok = sb("tok", [P, 1], F32)
        tok_i = sb("tok_i", [P, 1], I32)
        st = sb("st", [P, 2, 6], F32)
        mv = sb("mv", [P, 2], F32)
        ve = sb("ve", [P, 1], F32)
        neg_half = sb("neg_half", [P, 1], F32)
        rstd = sb("rstd", [P, 1], F32)
        mx = sb("mx", [P, 2], F32)
        nmx = sb("nmx", [P, 2], F32)
        psm = sb("psm", [P, 2], F32)
        sc = sb("sc", [P, 2], F32)
        lg = sb("lg", [P, E], F32)
        v8 = sb("v8", [P, 2, 8], F32)
        i8 = sb("i8", [P, 8], U32)
        i4 = sb("i4", [P, TOPK], F32)
        nv0 = sb("nv0", [P, 2], F32)
        oh = sb("oh", [P, 2, TOPK, E], F32)
        mask = sb("mask", [P, 2, E], F32)
        seen = sb("seen", [P, E], F32)
        rk = sb("rk", [P, E], F32)
        junk = sb("junk", [P, TOPK, E], F32)
        dest_f = sb("dest_f", [P, TOPK], F32)
        dest = sb("dest", [P, 2, TOPK], U32)
        ex = sb("ex", [P, 2, TOPK], F32)
        es = sb("es", [P, 2], F32)
        er = sb("er", [P, 1], F32)
        wt = sb("wt", [P, TOPK], F32)
        pack = sb("pack", [P, 2, TOPK, 4], I32)
        ncol = sb("ncol", [E, 4], F32)
        ge = sb("ge", [E, MAXT], F32)
        iota_t = sb("iota_t", [E, MAXT], F32)
        iota_ti = sb("iota_ti", [E, MAXT], I32)
        rowf = sb("rowf", [1, MAXT], F32)
        padding = xs2[:, :, :].rearrange("p a b -> p (a b)").bitcast(I32).rearrange("p (r c) -> p r c", c=4)
        wqk_in = prob[:, 0, :].rearrange("p (w c) -> p w c", w=2)
        gate_in = prob[0:E, 1, :]

        psE = psum("psE", [P, 2 * HALF], F32)
        psM = psum("psM", [P, 2 * HALF], F32)
        psT = psum("psT", [P, 2 * HALF], F32)
        psQ = psum("psQ", [P, HALF], F32)
        psR = psum("psR", [P, HALF], F32)
        psT16 = psT[:, :].bitcast(F16).rearrange("p (a b) -> p a b", a=2)
        wide = [psE, psM]
        quarter = [psM[:, 0:HALF], psM[:, HALF:], psE[:, 0:HALF], psE[:, HALF:]]

        s_x = [sem(f"x_in{t}") for t in range(NT)]
        s_ctx = sem("ctx_in")
        s_past = sem("waits_passed")
        s_small = sem("small_in")
        s_const = sem("consts")
        s_padfill = sem("pad_filled")
        s_padout = sem("pad_stored")
        s_ready = sem("dve_consts")
        s_wT = sem("w_transposed")
        s_wTev = sem("w_evacuated")
        s_x2out = [sem(f"x2_out{t}") for t in range(NT)]
        s_xnout = [sem(f"xn_out{t}") for t in range(2)]
        s_slotout = [sem(f"slot_out{t}") for t in range(2)]
        s_cT = sem("ctx_transposed")
        s_cTev = sem("ctxT_evacuated")
        s_qk = sem("qk_done")
        s_qkev = sem("qk_evacuated")
        s_E = sem("energy_done")
        s_nmx = sem("negmax_ready")
        s_exp = sem("exp_done")
        s_sc = sem("prob_scale_ready")
        s_ahi = sem("prob_hi")
        s_alo = sem("prob_lo")
        s_AT = sem("prob_transposed")
        s_AThi = sem("probT_hi")
        s_ATlo = sem("probT_lo")
        s_var = sem("variance_ready")
        s_rstd = sem("rstd_ready")
        s_xs = sem("ln1_ready")
        s_xhi = sem("ln1_hi")
        s_xlo = sem("ln1_lo")
        s_xT = sem("ln1_transposed")
        s_xTev = sem("ln1T_evacuated")
        s_xm = sem("xm_done")
        s_x2 = sem("x2_ready")
        s_xs2 = sem("ln2_ready")
        s_hi2 = sem("ln2_hi")
        s_lo2 = sem("ln2_lo")
        s_x2T = sem("ln2_transposed")
        s_x2Tev = sem("ln2T_evacuated")
        s_lgt = sem("logits_done")
        s_lgev = sem("logits_read")
        s_nv0 = sem("top1_ready")
        s_ex = sem("weights_exp")
        s_mask = sem("mask_ready")
        s_rank = sem("rank_done")
        s_seen = sem("seen_ready")
        s_pack = sem("pack_ready")
        s_dve = sem("dve_chain")
        s_tail = sem("tail_pe")
        s_tailv = sem("tail_dve")
        block = ctx.enter_context(nc.Block())

        @block.sync
        def _(sp):
            for t in range(2):
                sp.sem_inc(s_xnout[t], 16)
            sp.dma_start(wqk_in[:, 0, :], g["Wq"]).then_inc(s_small, 16)
            sp.dma_start(wqk_in[:, 1, :], g["Wk"]).then_inc(s_small, 16)
            sp.dma_start(gate_in, g["gate_w"]).then_inc(s_small, 16)
            sp.dma_start(bqk[:, 0:1], g["bq"].rearrange("(d o) -> d o", o=1)).then_inc(s_small, 16)
            sp.dma_start(bqk[:, 1:2], g["bk"].rearrange("(d o) -> d o", o=1)).then_inc(s_small, 16)
            sp.dma_start(gb[:], g["gate_b"].rearrange("(o e) -> o e", o=1).to_broadcast([P, E])).then_inc(s_small, 16)
            sp.dma_start(cx[:], ctx_in[0].rearrange("(t p) c -> p t c", p=P)).then_inc(s_ctx, 16)
            for t in range(NT):
                sp.dma_start(xr[:, t, :], x_rows[0, t]).then_inc(s_x[t], 16)
            sp.wait_ge(s_padfill, 2)
            half = SLOTS // P // 2
            for part in range(2):
                sp.dma_start(slots[0:SLOTS, :].rearrange("(p r) c -> p r c", p=P)[:, part * half:(part + 1) * half, :],
                             padding).then_inc(s_padout, 16)
            sp.dma_start(slots[SLOTS:SLOTS + 2 * P, :].rearrange("(o r) c -> o r c", o=1),
                         padding[0:1, 0:2 * P, :]).then_inc(s_padout, 16)
            zero = x2T[:, :, :].rearrange("p k q -> p (k q)")
            sp.dma_start(xn_rows[T // P], zero.bitcast(F16)).then_inc(s_padout, 16)
            sp.dma_start(acc_rows[T // P], zero).then_inc(s_padout, 16)
            with sp.Fori(0, B) as b:
                with sp.If(b < B - 1):
                    sp.wait_ge(s_cT, b * NT + NT)
                    sp.dma_start(cx[:], ctx_in[at(nc, b + 1, B - 1)].rearrange("o (t p) c -> p (o t) c", p=P)).then_inc(s_ctx, 16)
                for t in range(NT):
                    sp.wait_ge(s_x2, b * NT + t + 1)
                    sp.dma_start(acc_rows[bass.ds(b * NT + t, 1)].rearrange("o p h -> (o p) h"), xr[:, t, :]).then_inc(s_x2out[t], 16)
                    sp.wait_ge(s_lo2, b * NT + t + 1)
                    sp.dma_start(xn_rows[bass.ds(b * NT + t, 1)].rearrange("o p h -> (o p) h"),
                                 x2h[:, t % 2].rearrange("p a h -> p (a h)")).then_inc(s_xnout[t % 2], 16)
                    with sp.If(b < B - 1):
                        sp.wait_ge(s_x2out[t], 16 * b + 16)
                        sp.dma_start(xr[:, t, :], x_rows[at(nc, b + 1, B - 1), t].rearrange("o p h -> (o p) h")).then_inc(s_x[t], 16)
            for t in range(NT):
                sp.wait_ge(s_x2out[t], 16 * B)
            for t in range(2):
                sp.wait_ge(s_xnout[t], 16 * (B * NT // 2 + 1))

        @block.gpsimd
        def _(pool):
            pool.memset(ident[:], 0.0).then_inc(s_const, 1)
            pool.memset(ident16[:], 0.0).then_inc(s_const, 1)
            pool.memset(ones[:], 1.0).then_inc(s_const, 1)
            pool.memset(before[:], 1.0).then_inc(s_const, 1)
            pool.memset(upto[:], 1.0).then_inc(s_const, 1)
            pool.memset(seen[:], 0.0).then_inc(s_const, 1)
            pool.wait_ge(s_const, 6)
            for m in (ident, ident16):
                pool.affine_select(out=m[:], in_=m[:], compare_op=ALU.not_equal, fill=1.0, base=0,
                                   pattern=[[-1, P]], channel_multiplier=1).then_inc(s_const, 1)
            pool.affine_select(out=before[:], in_=before[:], compare_op=ALU.is_gt, fill=0.0, base=0,
                               pattern=[[1, P]], channel_multiplier=-1).then_inc(s_const, 1)
            pool.affine_select(out=upto[:], in_=upto[:], compare_op=ALU.is_ge, fill=0.0, base=0,
                               pattern=[[1, E]], channel_multiplier=-1).then_inc(s_const, 1)
            pool.iota(iota_i[:], pattern=[[1, E]], base=0, channel_multiplier=0).then_inc(s_const, 1)
            pool.iota(iota_ti[:], pattern=[[1, MAXT]], base=0, channel_multiplier=0).then_inc(s_const, 1)
            pool.iota(tok_i[:], pattern=[[0, 1]], base=0, channel_multiplier=1).then_inc(s_const, 1)
            pool.memset(padding, 0).then_inc(s_const, 1)
            pool.memset(x2T[:], 0.0).then_inc(s_padfill, 1)
            pool.memset(neg_half[:], -0.5).then_inc(s_const, 1)
            pool.memset(pack[:], 0).then_inc(s_const, 1)
            pool.wait_ge(s_const, 16)
            pool.iota(padding[:, :, 0].rearrange("p (a l) -> p a l", l=P), pattern=[[0, padding.shape[1] // P], [1, P]],
                      base=T, channel_multiplier=0).then_inc(s_padfill, 1)
            pool.wait_ge(s_padout, 16 * 5)
            def inverse_root(nth):
                pool.wait_ge(s_var, nth)
                pool.tensor_tensor(out=rstd[:], in0=ve[:], in1=neg_half[:], op=ALU.pow).then_inc(s_rstd, 1)

            with pool.Fori(0, B) as b:
                for m in range(NT):
                    inverse_root(2 * NT * b + m + 1)
                for t in range(NT + 3):
                    if t < NT:
                        inverse_root(2 * NT * b + NT + t + 1)
                    if t >= 3:
                        n = t - 3
                        alone(pool, s_pack, b * NT + n + 1, s_past)
                        for k in range(TOPK):
                            pool.indirect_dma_start(
                                out=slots[:, :], out_offset=bass.IndirectOffsetOnAxis(dest[:, n % 2, k:k + 1], 0),
                                in_=pack[:, n % 2, k, :], in_offset=None).then_inc(s_slotout[n % 2], 16)
            for t in range(2):
                pool.wait_ge(s_slotout[t], 16 * TOPK * (B * NT // 2))

        @block.scalar
        def _(act):
            for n in range(2 * KC + KH):
                act.wait_ge(s_wT, n + 1)
                if n < 2 * KC:
                    act.activation(WT[:, n // KC, n % KC, :], psT[:, n % 2 * HALF:n % 2 * HALF + D], ACT.Copy).then_inc(s_wTev, 1)
                else:
                    act.activation(gateT[:, n - 2 * KC, :], psT[:, n % 2 * HALF:n % 2 * HALF + E], ACT.Copy).then_inc(s_wTev, 1)
            act.wait_ge(s_padout, 16 * 5)
            with act.Fori(0, B) as b:
                t0 = b * NT
                for t in range(NT):
                    act.wait_ge(s_cT, t0 + t + 1)
                    act.activation(cxT[:, :, t * P:(t + 1) * P],
                                   psT[:, t % 2 * HALF:(t % 2 + 1) * HALF].rearrange("p (c q) -> p c q", c=KC),
                                   ACT.Copy).then_inc(s_cTev, 1)
                act.wait_ge(s_xs, t0 + 1)
                act.activation(xnh[:, 0, :], xs[:], ACT.Copy, scale=S_ROWS).then_inc(s_xhi, 1)
                for m in range(NT + 1):
                    if m < NT:
                        act.wait_ge(s_nmx, t0 + m + 1)
                        act.activation(prob[:, m % 2, :], wide[m % 2][:], ACT.Exp, bias=nmx[:, m % 2:m % 2 + 1],
                                       accum_out=psm[:, m % 2:m % 2 + 1]).then_inc(s_exp, 1)
                        act.wait_ge(s_xT, t0 + m + 1)
                        act.activation(XT[:, :, :, m * P:(m + 1) * P],
                                       psT16.rearrange("p a (k q) -> p a k q", q=P), ACT.Copy).then_inc(s_xTev, 1)
                    if m < NT - 1:
                        act.wait_ge(s_xs, t0 + m + 2)
                        act.activation(xnh[:, 0, :], xs[:], ACT.Copy, scale=S_ROWS).then_inc(s_xhi, 1)
                    if m < NT:
                        act.wait_ge(s_sc, t0 + m + 1)
                        act.activation(ah[:, m % 2, 0, :], prob[:, m % 2, :], ACT.Copy,
                                       scale=sc[:, m % 2:m % 2 + 1]).then_inc(s_ahi, 1)
                    if m >= 1:
                        act.wait_ge(s_AT, t0 + m)
                        act.activation(AT[:, 0, :, (m - 1) * P:m * P],
                                       psT16[:, 0, :].rearrange("p (k q) -> p k q", q=P), ACT.Copy).then_inc(s_AThi, 1)
                for t in range(NT + 2):
                    if t < NT:
                        act.wait_ge(s_xnout[t % 2], 16 * (b * (NT // 2) + t // 2 + 1))
                        act.wait_ge(s_xs2, t0 + t + 1)
                        act.activation(x2h[:, t % 2, 0, :], xs2[:, t % 2, :], ACT.Copy, scale=S_ROWS).then_inc(s_hi2, 1)
                    if 1 <= t <= NT:
                        act.wait_ge(s_x2T, t0 + t)
                        act.activation(x2T[:], psT[:, :].rearrange("p (k q) -> p k q", q=P), ACT.Copy).then_inc(s_x2Tev, 1)
                    if t >= 2:
                        n = t - 2
                        act.wait_ge(s_nv0, t0 + n + 1)
                        act.activation(ex[:, n % 2, :], v8[:, n % 2, 0:TOPK], ACT.Exp, bias=nv0[:, n % 2:n % 2 + 1],
                                       accum_out=es[:, n % 2:n % 2 + 1]).then_inc(s_ex, 1)

        @block.tensor
        def _(pe):
            pe.wait_ge(s_const, 10)
            pe.wait_ge(s_small, 16 * 6)
            for n in range(2 * KC + KH):
                if n >= 2:
                    pe.wait_ge(s_wTev, n - 1)
                dst = psT[:, n % 2 * HALF:]
                if n < 2 * KC:
                    pe.transpose(dst[:, 0:D], wqk_in[:, n // KC, n % KC * P:(n % KC + 1) * P], ident[:]).then_inc(s_wT, 1)
                else:
                    k = n - 2 * KC
                    pe.transpose(dst[:, 0:E], gate_in[:, k * P:(k + 1) * P], ident[0:E, 0:E]).then_inc(s_wT, 1)
            pe.wait_ge(s_wTev, 2 * KC + KH)
            pe.wait_ge(s_ready, 1)
            with pe.Fori(0, B) as b:
                t0 = b * NT
                pe.wait_ge(s_ctx, 16 * b + 16)
                for t in range(NT):
                    if t >= 2:
                        pe.wait_ge(s_cTev, t0 + t - 1)
                    for c in range(KC):
                        op = pe.transpose(psT[:, t % 2 * HALF + c * P:t % 2 * HALF + (c + 1) * P],
                                          cx[:, t, c * P:(c + 1) * P], ident[:])
                    op.then_inc(s_cT, 1)
                pe.wait_ge(s_cTev, t0 + NT)
                for n in range(4):
                    for c in range(KC):
                        op = pe.matmul(quarter[n], WT[:, n // 2, c, :], cxT[:, c, n % 2 * HALF:(n % 2 + 1) * HALF],
                                       start=c == 0, stop=c == KC - 1)
                    op.then_inc(s_qk, 1)
                pe.wait_ge(s_qkev, b * 4 + 4)
                for m in range(NT + 1):
                    if m < NT:
                        if m >= 2:
                            pe.wait_ge(s_exp, t0 + m - 1)
                        for h in range(2):
                            op = pe.matmul(wide[m % 2][:, h * HALF:(h + 1) * HALF], qk[:, 0, m * P:(m + 1) * P],
                                           qk[:, 1, h * HALF:(h + 1) * HALF], start=True, stop=True)
                        op.then_inc(s_E, 1)
                        pe.wait_ge(s_xlo, t0 + m + 1)
                        if m == 1:
                            pe.wait_ge(s_xTev, t0 + 1)
                        if m >= 2:
                            pe.wait_ge(s_AThi, t0 + m - 1)
                            pe.wait_ge(s_ATlo, t0 + m - 1)
                        for a in range(2):
                            for k in range(KH):
                                op = pe.transpose(psT16[:, a, k * P:(k + 1) * P], xnh[:, a, k * P:(k + 1) * P], ident16[:])
                        op.then_inc(s_xT, 1)
                    if m >= 1:
                        pe.wait_ge(s_alo, t0 + m)
                        if m < NT:
                            pe.wait_ge(s_xTev, t0 + m + 1)
                        else:
                            pe.wait_ge(s_AThi, t0 + NT - 1)
                            pe.wait_ge(s_ATlo, t0 + NT - 1)
                        for a in range(2):
                            for k in range(KH):
                                op = pe.transpose(psT16[:, a, k * P:(k + 1) * P], ah[:, (m - 1) % 2, a, k * P:(k + 1) * P], ident16[:])
                        op.then_inc(s_AT, 1)
                pe.wait_ge(s_xTev, t0 + NT)
                pe.wait_ge(s_AThi, t0 + NT)
                pe.wait_ge(s_ATlo, t0 + NT)
                for t in range(NT + 3):
                    if t < NT:
                        if t >= 2:
                            pe.wait_ge(s_x2, t0 + t - 1)
                        for h in range(2):
                            for k in range(KH):
                                for n, (a, c) in enumerate(((0, 0), (0, 1), (1, 0))):
                                    op = pe.matmul(wide[t % 2][:, h * HALF:(h + 1) * HALF], XT[:, a, k, t * P:(t + 1) * P],
                                                   AT[:, c, k, h * HALF:(h + 1) * HALF],
                                                   start=k == 0 and n == 0, stop=k == KH - 1 and n == 2)
                        op.then_inc(s_xm, 1)
                    if t >= 3:
                        n = t - 3
                        pe.wait_ge(s_mask, t0 + n + 1)
                        pe.wait_ge(s_seen, t0 + n + 1)
                        pe.matmul(psQ[:, 0:E], before[:], mask[:, n % 2, :], start=True, stop=False)
                        pe.matmul(psQ[:, 0:E], ones[:], seen[:], start=False, stop=True).then_inc(s_rank, 1)
                    if 2 <= t < NT + 2:
                        n = t - 2
                        pe.wait_ge(s_x2Tev, t0 + n + 1)
                        if n >= 1:
                            pe.wait_ge(s_lgev, t0 + n)
                        for k in range(KH):
                            op = pe.matmul(psR[:, 0:E], x2T[:, k, :], gateT[:, k, :], start=k == 0, stop=k == KH - 1)
                        op.then_inc(s_lgt, 1)
                    if 1 <= t < NT + 1:
                        n = t - 1
                        pe.wait_ge(s_xs2, t0 + n + 1)
                        for k in range(KH):
                            op = pe.transpose(psT[:, k * P:(k + 1) * P], xs2[:, n % 2, k * P:(k + 1) * P], ident[:])
                        op.then_inc(s_x2T, 1)
            pe.wait_ge(s_seen, B * NT + 1)
            pe.matmul(psQ[0:E, 0:1], seen[:], ones[:, 0:1], start=True, stop=True).then_inc(s_tail, 1)
            pe.wait_ge(s_tailv, 1)
            pe.matmul(psR[0:E, 0:1], upto[:], ncol[:, 0:1], start=True, stop=True).then_inc(s_tail, 1)
            pe.wait_ge(s_tailv, 2)
            pe.matmul(psE[0:1, 0:E], ncol[:, 0:1], upto[:], start=True, stop=True).then_inc(s_tail, 1)
            pe.matmul(psM[0:1, 0:MAXT], ones[0:E, 0:1], ge[:], start=True, stop=True).then_inc(s_tail, 1)

        @block.vector
        def _(dve):
            def link(tally, ins):
                tally.inc(ins)
                dve.wait_ge(tally.sem, tally.now())

            def layernorm(tally, out, src, ready, nth):
                for h in range(2):
                    tally.inc(dve.bn_stats(st[:, h, :], src[:, h * HALF:(h + 1) * HALF]))
                alone(dve, tally.sem, tally.now(), s_past)
                link(tally, dve.bn_aggr(mv[:], st[:, :, :]))
                dve.tensor_scalar(ve[:], mv[:, 1:2], EPS, None, ALU.add).then_inc(s_var, 1)
                dve.wait_ge(s_rstd, nth)
                dve.tensor_scalar(out, src, mv[:, 0:1], rstd[:], ALU.subtract, ALU.mult).then_inc(ready, 1)

            first = Tally(s_dve)
            dve.wait_ge(s_const, 13)
            link(first, dve.tensor_copy(iota_e[:], iota_i[:]))
            link(first, dve.tensor_scalar(ebase[:], iota_e[:], float(T), None, ALU.mult))
            link(first, dve.tensor_copy(iota_t[:], iota_ti[:]))
            link(first, dve.tensor_copy(tok[:], tok_i[:]))
            dve.memset(lg[:], 0.0).then_inc(s_ready, 1)
            dve.memset(psm[:], 0.0).then_inc(s_seen, 1)
            dve.wait_ge(s_small, 16 * 6)
            dve.wait_ge(s_padout, 16 * 5)
            PER_BATCH = 3 * NT * 2 + 20 * NT
            with dve.Fori(0, B) as b:
                t0 = b * NT
                v = Tally(s_dve, b * PER_BATCH + first.n)
                dve.wait_ge(s_x[0], 16 * b + 16)
                layernorm(v, xs[:], xr[:, 0, :], s_xs, 2 * t0 + 1)
                dve.wait_ge(s_xhi, t0 + 1)
                dve.scalar_tensor_tensor(out=xnh[:, 1, :], in0=xs[:], scalar=S_ROWS, in1=xnh[:, 0, :],
                                         op0=ALU.mult, op1=ALU.subtract).then_inc(s_xlo, 1)
                for n in range(4):
                    dve.wait_ge(s_qk, b * 4 + n + 1)
                    dve.tensor_scalar(qk[:, n // 2, n % 2 * HALF:(n % 2 + 1) * HALF], quarter[n],
                                      bqk[:, n // 2:n // 2 + 1], None, ALU.add).then_inc(s_qkev, 1)
                for m in range(NT + 1):
                    j = m % 2
                    if m < NT:
                        dve.wait_ge(s_E, t0 + m + 1)
                        link(v, dve.reduce_max(mx[:, j:j + 1], wide[j][:], axis=AX_X))
                        dve.tensor_scalar(nmx[:, j:j + 1], mx[:, j:j + 1], -1.0, None, ALU.mult).then_inc(s_nmx, 1)
                    if m < NT - 1:
                        dve.wait_ge(s_x[m + 1], 16 * b + 16)
                        layernorm(v, xs[:], xr[:, m + 1, :], s_xs, 2 * t0 + m + 2)
                    if m < NT:
                        dve.wait_ge(s_exp, t0 + m + 1)
                        link(v, dve.reciprocal(sc[:, j:j + 1], psm[:, j:j + 1]))
                        dve.tensor_scalar(sc[:, j:j + 1], sc[:, j:j + 1], S_PROB, None, ALU.mult).then_inc(s_sc, 1)
                    if m < NT - 1:
                        dve.wait_ge(s_xhi, t0 + m + 2)
                        dve.scalar_tensor_tensor(out=xnh[:, 1, :], in0=xs[:], scalar=S_ROWS, in1=xnh[:, 0, :],
                                                 op0=ALU.mult, op1=ALU.subtract).then_inc(s_xlo, 1)
                    if m >= 1:
                        dve.wait_ge(s_AT, t0 + m)
                        dve.tensor_copy(AT[:, 1, :, (m - 1) * P:m * P],
                                        psT16[:, 1, :].rearrange("p (k q) -> p k q", q=P)).then_inc(s_ATlo, 1)
                    if m < NT:
                        dve.wait_ge(s_ahi, t0 + m + 1)
                        dve.wait_ge(s_sc, t0 + m + 1)
                        dve.scalar_tensor_tensor(out=ah[:, j, 1, :], in0=prob[:, j, :], scalar=sc[:, j:j + 1],
                                                 in1=ah[:, j, 0, :], op0=ALU.mult, op1=ALU.subtract).then_inc(s_alo, 1)
                for t in range(NT + 3):
                    if t < NT:
                        j = t % 2
                        dve.wait_ge(s_xm, t0 + t + 1)
                        dve.scalar_tensor_tensor(out=xr[:, t, :], in0=wide[j][:], scalar=1.0 / (S_ROWS * S_PROB),
                                                 in1=xr[:, t, :], op0=ALU.mult, op1=ALU.add).then_inc(s_x2, 1)
                        dve.wait_ge(s_x2, t0 + t + 1)
                        if t >= 2:
                            dve.wait_ge(s_x2T, t0 + t - 1)
                        layernorm(v, xs2[:, j, :], xr[:, t, :], s_xs2, 2 * t0 + NT + t + 1)
                    if 2 <= t < NT + 2:
                        n = t - 2
                        j = n % 2
                        dve.wait_ge(s_lgt, t0 + n + 1)
                        dve.tensor_tensor(lg[:], psR[:, 0:E], gb[:], ALU.add).then_inc(s_lgev, 1)
                        alone(dve, s_lgev, t0 + n + 1, s_past)
                        link(v, dve.max(v8[:, j, :], lg[:]))
                        dve.tensor_scalar(nv0[:, j:j + 1], v8[:, j, 0:1], -1.0, None, ALU.mult).then_inc(s_nv0, 1)
                        link(v, dve.max_index(i8[:], v8[:, j, :], lg[:]))
                        link(v, dve.tensor_copy(i4[:], i8[:, 0:TOPK]))
                        for k in range(TOPK):
                            v.inc(dve.tensor_scalar(oh[:, j, k, :], iota_e[:], i4[:, k:k + 1], None, ALU.is_equal))
                        dve.wait_ge(v.sem, v.now())
                        dve.tensor_reduce(mask[:, j, :], oh[:, j].rearrange("p k e -> p e k"), AX_X, ALU.add).then_inc(s_mask, 1)
                    if t >= 3:
                        n = t - 3
                        j = n % 2
                        dve.wait_ge(s_rank, t0 + n + 1)
                        link(v, dve.tensor_tensor(rk[:], psQ[:, 0:E], ebase[:], ALU.add))
                        for k in range(TOPK):
                            v.inc(dve.tensor_tensor_reduce(out=junk[:, k, :], in0=oh[:, j, k, :], in1=rk[:], scale=1.0, scalar=0.0,
                                                           op0=ALU.mult, op1=ALU.add, accum_out=dest_f[:, k:k + 1]))
                        alone(dve, v.sem, v.now(), s_past)
                        if n < 2:
                            with dve.If(b > 0):
                                alone(dve, s_slotout[j], 16 * TOPK * (NT // 2) * b, s_past)
                        else:
                            dve.wait_ge(s_slotout[j], 16 * TOPK * (b * (NT // 2) + n // 2))
                        v.inc(dve.tensor_copy(dest[:, j, :], dest_f[:]))
                        dve.wait_ge(s_ex, t0 + n + 1)
                        link(v, dve.reciprocal(er[:], es[:, j:j + 1]))
                        link(v, dve.tensor_scalar(wt[:], ex[:, j, :], er[:], None, ALU.mult))
                        v.inc(dve.tensor_copy(pack[:, j, :, 1].bitcast(F32), wt[:]))
                        v.inc(dve.tensor_scalar(pack[:, j, :, 2].bitcast(F32), wt[:], 1.0 / (S_ACT * S_W), None, ALU.mult))
                        v.inc(dve.tensor_copy(pack[:, j, :, 0], tok[:].to_broadcast([P, TOPK])))
                        dve.wait_ge(v.sem, v.now())
                        dve.tensor_tensor(seen[:], seen[:], mask[:, j, :], ALU.add).then_inc(s_seen, 1)
                        dve.tensor_scalar(tok[:], tok[:], float(P), None, ALU.add).then_inc(s_pack, 1)
                        dve.wait_ge(s_pack, t0 + n + 1)
                    if t < NT:
                        j = t % 2
                        dve.wait_ge(s_hi2, t0 + t + 1)
                        dve.scalar_tensor_tensor(out=x2h[:, j, 1, :], in0=xs2[:, j, :], scalar=S_ROWS, in1=x2h[:, j, 0, :],
                                                 op0=ALU.mult, op1=ALU.subtract).then_inc(s_lo2, 1)
                assert v.n == PER_BATCH
            z = Tally(s_dve, first.n + B * PER_BATCH)
            dve.wait_ge(s_tail, 1)
            link(z, dve.tensor_copy(ncol[:, 3:4], psQ[0:E, 0:1]))
            link(z, dve.tensor_scalar(ge[:, 0:T // P], iota_t[:, 0:T // P], float(P), ncol[:, 3:4], ALU.mult, ALU.is_lt))
            link(z, dve.reduce_sum(ncol[:, 2:3], ge[:, 0:T // P], axis=AX_X))
            dve.tensor_scalar(ncol[:, 0:1], ncol[:, 2:3], float(MIN_TILES), None, ALU.max).then_inc(s_tailv, 1)
            dve.wait_ge(s_tailv, 1)
            link(z, dve.tensor_scalar(ncol[:, 1:2], ncol[:, 0:1], -float(P), float(T), ALU.mult, ALU.add))
            dve.wait_ge(s_tail, 2)
            link(z, dve.tensor_copy(ncol[:, 2:3], psR[0:E, 0:1]))
            link(z, dve.tensor_scalar(ge[:], iota_t[:], ncol[:, 2:3], ncol[:, 1:2], ALU.is_ge, ALU.mult))
            dve.memset(tile_start[:], 0).then_inc(s_tailv, 1)
            dve.wait_ge(s_tailv, 2)
            dve.wait_ge(s_tail, 3)
            dve.tensor_copy(tile_start[0:1, 1:E + 1], psE[0:1, 0:E]).then_inc(s_tailv, 1)
            dve.wait_ge(s_tail, 4)
            link(z, dve.scalar_tensor_tensor(out=rowf[:], in0=iota_t[0:1, :], scalar=float(P), in1=psM[0:1, 0:MAXT],
                                             op0=ALU.mult, op1=ALU.add))
            dve.tensor_copy(slot_row[:], rowf[:]).then_inc(s_tailv, 1)
            dve.wait_ge(s_tailv, 4)


def experts(nc, g):
    H, E, I, T = g["H"], g["E"], g["I"], g["T"]
    KH, KI, HALF, NCHUNK, MAXT = g["KH"], g["KI"], g["HALF"], g["NCHUNK"], g["MAXT"]
    slots, xn_tab, acc = g["slots"], g["xn_tab"], g["acc"]
    ident16, tile_start, slot_row = g["ident16"], g["tile_start"], g["slot_row"]
    w_dram = [g["w_gate"].rearrange("e (k p) n -> e p k n", p=P), g["w_up"].rearrange("e (k p) n -> e p k n", p=P),
              g["w_down"].rearrange("e (k p) n -> e p k n", p=P)]
    RING = 3
    PAIRS = E // 2
    PER_W = NCHUNK // 3
    CUT = [[0, 1], [2, 3], [4, 5]]
    LOAD = [[3, 4], [5], [6, 7, 8]]
    assert NCHUNK == 6 and len(CUT) == MIN_TILES
    PASSES = ((0, 0), (0, 1), (1, 0))

    with ExitStack() as ctx:
        def sb(name, shape, dt):
            return ctx.enter_context(nc.sbuf_tensor(name, shape, dt))

        def psum(name, shape, dt):
            return ctx.enter_context(nc.psum_tensor(name, shape, dt))

        def sem(name):
            return ctx.enter_context(nc.semaphore(name))

        W = sb("W", [P, 2, 2, NCHUNK * CHUNK], F16)
        stage = sb("stage", [P, RING, CHUNK], F32)
        bias = sb("bias", [P, 2, 2 * I + H], F32)
        idxg = sb("idxg", [P, 4], I32)
        idxs = sb("idxs", [P, 4], I32)
        xg = sb("xg", [P, 2 * H], F16)
        xT = sb("xT", [P, 2, KH, P], F16)
        gt = sb("gt", [P, I], F32)
        sg = sb("sg", [P, I], F32)
        up = sb("up", [P, I], F32)
        av = sb("av", [P, I], F32)
        ahl = sb("ahl", [P, 2, I], F16)
        aT = sb("aT", [P, 2, KI, P], F16)
        y = sb("y", [P, H], F32)
        psG = psum("psG", [P, HALF], F32)
        psU = psum("psU", [P, HALF], F32)
        psX = psum("psX", [P, 2 * KH * P], F16)
        psA = psum("psA", [P, 2 * KI * P], F16)
        psY = psum("psY", [P, 2 * HALF], F32)

        s_past = sem("waits_passed")
        s_stage = [sem(f"chunk_in{r}") for r in range(RING)]
        s_bias = sem("bias_in")
        s_idxg = sem("gather_idx_in")
        s_idxs = sem("scatter_idx_in")
        s_xg = sem("rows_gathered")
        s_scat = sem("rows_added")
        s_added = sem("tile_added")
        s_whi = sem("weights_hi")
        s_wlo = sem("weights_lo")
        s_G = sem("gate_done")
        s_U = sem("up_done")
        s_X = sem("x_transposed")
        s_A = sem("act_transposed")
        s_Y = sem("down_done")
        s_gread = sem("gate_read")
        s_gmin = sem("gate_clipped")
        s_sig = sem("sigmoid_done")
        s_glu = sem("glu_done")
        s_uread = sem("up_read")
        s_uclip = sem("up_clipped")
        s_act = sem("act_ready")
        s_ahi = sem("act_hi")
        s_alo = sem("act_lo")
        s_xTev = sem("xT_evacuated")
        s_aTev = sem("aT_evacuated")
        s_y0 = sem("y_weighted")
        s_y = sem("y_ready")
        block = ctx.enter_context(nc.Block())

        def start_of(eng, e):
            return eng.value_load(tile_start[0:1, at(nc, e, E)], min_val=0, max_val=MAXT - 4)

        def chunk_src(q_expert, c):
            w = w_dram[c // PER_W]
            n = CHUNK // w.shape[3]
            k0 = c % PER_W * n
            return w[at(nc, q_expert, E - 1), :, k0:k0 + n, :].rearrange("o p k n -> (o p) k n")

        def load_chunk(sp, e, c):
            view = stage[:, c % RING, :].rearrange("p (k n) -> p k n", n=w_dram[c % NCHUNK // PER_W].shape[3])
            sp.dma_start(view, chunk_src(e + c // NCHUNK, c % NCHUNK)).then_inc(s_stage[c % RING], 16)

        def load_bias(sp, e, par):
            for lo, hi, src in ((0, I, g["b_gate"]), (I, 2 * I, g["b_up"]), (2 * I, 2 * I + H, g["b_down"])):
                sp.dma_start(bias[:, par, lo:hi], src[at(nc, e, E - 1), :].to_broadcast([P, hi - lo])).then_inc(s_bias, 16)

        def load_slots(sp, dst, i, done):
            row = sp.value_load(slot_row[0:1, at(nc, i, MAXT - 1)], min_val=0, max_val=slots.shape[0] - P)
            sp.dma_start(dst[:], slots[bass.ds(row, P), :]).then_inc(done, 16)

        @block.sync
        def _(sp):
            load_slots(sp, idxg, 0, s_idxg)
            for c in range(RING):
                load_chunk(sp, 0, c)
            load_bias(sp, 0, 0)
            sp.wait_ge(s_xg, 16)
            load_slots(sp, idxg, 1, s_idxg)
            for c in range(RING, NCHUNK + RING):
                sp.wait_ge(s_wlo, c - RING + 1)
                load_chunk(sp, 0, c)

            def step(i, e, t0, j, more, prev_guard):
                def prev():
                    alone(sp, s_added, i, s_past)
                    load_slots(sp, idxs, i - 1, s_idxs)
                if prev_guard is None:
                    prev()
                else:
                    with sp.If(prev_guard):
                        prev()
                sp.wait_ge(s_xg, 16 * i + 32)
                load_slots(sp, idxg, i + 2, s_idxg)
                if j is not None:
                    def loads():
                        for c in LOAD[j]:
                            alone(sp, s_wlo, NCHUNK * e + NCHUNK + c - RING + 1, s_past)
                            load_chunk(sp, e + 1, c)
                    if more[j] is None:
                        loads()
                    else:
                        with sp.If(more[j]):
                            loads()

            with sp.Fori(0, PAIRS) as pair:
                for par in range(2):
                    e = pair * 2 + par
                    t0, t1 = start_of(sp, e), start_of(sp, e + 1)
                    some = pair < PAIRS - 1
                    more = [None if par == 0 else some] * 2 + [some]
                    for j in range(MIN_TILES):
                        step(t0 + j, e, t0, j, more, pair > 0 if par == 0 and j == 0 else None)
                    if par == 0:
                        sp.wait_ge(s_y, t0 + 1)
                        load_bias(sp, e + 1, 1 - par)
                    else:
                        with sp.If(some):
                            sp.wait_ge(s_y, t0 + 1)
                            load_bias(sp, e + 1, 1 - par)
                    with sp.If(t1 > t0 + MIN_TILES):
                        with sp.Fori(t0 + MIN_TILES, t1) as i:
                            step(i, e, t0, None, None, None)
            tt = start_of(sp, E)
            alone(sp, s_added, tt, s_past)
            load_slots(sp, idxs, tt - 1, s_idxs)
            alone(sp, s_idxg, 16 * tt + 32, s_past)

        @block.gpsimd
        def _(pool):
            def gather(i):
                alone(pool, s_idxg, 16 * i + 16, s_past)
                pool.indirect_dma_start(out=xg[:], out_offset=None, in_=xn_tab[:, :],
                                        in_offset=bass.IndirectOffsetOnAxis(idxg[:, 0:1].bitcast(U32), 0)).then_inc(s_xg, 16)

            def scatter(i):
                alone(pool, s_y, i + 1, s_past)
                pool.indirect_dma_start(out=acc[:, :], out_offset=bass.IndirectOffsetOnAxis(idxs[:, 0:1].bitcast(U32), 0),
                                        in_=y[:], in_offset=None, compute_op=ALU.add).then_inc(s_scat, 16)

            pool.sem_inc(s_added, 1)
            tt = start_of(pool, E)
            gather(0)
            pool.wait_ge(s_X, 1)
            gather(1)
            pool.wait_ge(s_X, 2)
            gather(2)
            scatter(0)
            with pool.Fori(2, tt + 1) as i:
                pool.wait_ge(s_X, i + 1)
                gather(i + 1)
                pool.wait_ge(s_scat, 16 * i - 16)
                pool.sem_inc(s_added, 1)
                scatter(i - 1)
            alone(pool, s_xg, 16 * tt + 32, s_past)
            alone(pool, s_scat, 16 * tt, s_past)

        @block.scalar
        def _(act):
            def cut(e, par, c, free=None):
                act.wait_ge(s_stage[c % RING], 32 * e + 16 * (c // RING) + 16)
                if free is not None:
                    free()
                act.activation(W[:, par, 0, c * CHUNK:(c + 1) * CHUNK], stage[:, c % RING, :], ACT.Copy, scale=S_W).then_inc(s_whi, 1)

            def evac_x(i):
                act.wait_ge(s_X, i + 1)
                act.activation(xT[:].rearrange("p a k q -> p (a k q)"), psX[:], ACT.Copy).then_inc(s_xTev, 1)

            def evac_a(i):
                act.wait_ge(s_A, i + 1)
                act.activation(aT[:].rearrange("p a k q -> p (a k q)"), psA[:], ACT.Copy).then_inc(s_aTev, 1)

            def weigh_y(i):
                act.wait_ge(s_idxs, 16 * i + 16)
                act.wait_ge(s_added, i + 1)
                act.wait_ge(s_Y, i + 1)
                act.activation(y[:], psY[:], ACT.Copy, scale=idxs[:, 2:3].bitcast(F32)).then_inc(s_y0, 1)

            act.sem_inc(s_y0, 1)
            for c in range(NCHUNK):
                cut(0, 0, c)
            evac_x(0)

            def step(i, e, par, t0, j, more, prev_guard):
                def guarded(guard, body):
                    if guard is None:
                        body()
                    else:
                        with act.If(guard):
                            body()

                def free_gate_up():
                    alone(act, s_U, t0, s_past)

                def cut_one(n):
                    c = CUT[j][n]
                    if c == 0:
                        guarded(prev_guard, free_gate_up)
                    if c == 2 * PER_W:
                        act.wait_ge(s_Y, t0 + 1)
                    cut(e + 1, 1 - par, c)

                if j is not None:
                    guarded(more, lambda: cut_one(0))
                act.wait_ge(s_gmin, i + 1)
                act.activation(sg[:], gt[:], ACT.Sigmoid, scale=ALPHA).then_inc(s_sig, 1)
                guarded(prev_guard, lambda: evac_a(i - 1))
                if j is not None:
                    guarded(more, lambda: cut_one(1))
                evac_x(i + 1)
                act.wait_ge(s_act, i + 1)
                act.activation(ahl[:, 0, :], av[:], ACT.Copy, scale=S_ACT).then_inc(s_ahi, 1)
                guarded(prev_guard, lambda: weigh_y(i - 1))

            with act.Fori(0, PAIRS) as pair:
                for par in range(2):
                    e = pair * 2 + par
                    t0, t1 = start_of(act, e), start_of(act, e + 1)
                    for j in range(MIN_TILES):
                        step(t0 + j, e, par, t0, j, pair < PAIRS - 1 if par else None,
                             pair > 0 if par == 0 and j == 0 else None)
                    with act.If(t1 > t0 + MIN_TILES):
                        with act.Fori(t0 + MIN_TILES, t1) as i:
                            step(i, e, par, t0, None, None, None)
            tt = start_of(act, E)
            evac_a(tt - 1)
            weigh_y(tt - 1)

        @block.vector
        def _(dve):
            def cut(e, par, c):
                dve.wait_ge(s_whi, NCHUNK * e + c + 1)
                dve.scalar_tensor_tensor(out=W[:, par, 1, c * CHUNK:(c + 1) * CHUNK], in0=stage[:, c % RING, :], scalar=S_W,
                                         in1=W[:, par, 0, c * CHUNK:(c + 1) * CHUNK], op0=ALU.mult, op1=ALU.subtract).then_inc(s_wlo, 1)

            def finish_y(i, par):
                dve.wait_ge(s_y0, i + 2)
                dve.scalar_tensor_tensor(out=y[:], in0=bias[:, par, 2 * I:], scalar=idxs[:, 1:2].bitcast(F32), in1=y[:],
                                         op0=ALU.mult, op1=ALU.add).then_inc(s_y, 1)

            for c in range(NCHUNK):
                cut(0, 0, c)

            def step(i, e, par, j, more, prev_guard):
                def guarded(guard, body):
                    if guard is None:
                        body()
                    else:
                        with dve.If(guard):
                            body()

                if j == 0:
                    dve.wait_ge(s_bias, 48 * e + 48)
                dve.wait_ge(s_G, i + 1)
                dve.scalar_tensor_tensor(out=gt[:], in0=psG[:], scalar=1.0 / (S_ROWS * S_W), in1=bias[:, par, 0:I],
                                         op0=ALU.mult, op1=ALU.add).then_inc(s_gread, 1)
                dve.wait_ge(s_gread, i + 1)
                dve.tensor_scalar(gt[:], gt[:], LIMIT, None, ALU.min).then_inc(s_gmin, 1)
                if j is not None:
                    guarded(more, lambda: cut(e + 1, 1 - par, CUT[j][0]))
                dve.wait_ge(s_sig, i + 1)
                dve.tensor_tensor(gt[:], gt[:], sg[:], ALU.mult).then_inc(s_glu, 1)
                dve.wait_ge(s_U, i + 1)
                dve.scalar_tensor_tensor(out=up[:], in0=psU[:], scalar=1.0 / (S_ROWS * S_W), in1=bias[:, par, I:2 * I],
                                         op0=ALU.mult, op1=ALU.add).then_inc(s_uread, 1)
                dve.wait_ge(s_uread, i + 1)
                dve.tensor_scalar(up[:], up[:], LIMIT, -LIMIT, ALU.min, ALU.max).then_inc(s_uclip, 1)
                dve.wait_ge(s_glu, i + 1)
                dve.wait_ge(s_uclip, i + 1)
                dve.scalar_tensor_tensor(out=av[:], in0=up[:], scalar=1.0, in1=gt[:], op0=ALU.add, op1=ALU.mult).then_inc(s_act, 1)
                if j is not None:
                    guarded(more, lambda: cut(e + 1, 1 - par, CUT[j][1]))
                dve.wait_ge(s_ahi, i + 1)
                dve.scalar_tensor_tensor(out=ahl[:, 1, :], in0=av[:], scalar=S_ACT, in1=ahl[:, 0, :],
                                         op0=ALU.mult, op1=ALU.subtract).then_inc(s_alo, 1)
                guarded(prev_guard, lambda: finish_y(i - 1, 1 - par if j == 0 else par))

            with dve.Fori(0, PAIRS) as pair:
                for par in range(2):
                    e = pair * 2 + par
                    t0, t1 = start_of(dve, e), start_of(dve, e + 1)
                    for j in range(MIN_TILES):
                        step(t0 + j, e, par, j, pair < PAIRS - 1 if par else None, pair > 0 if par == 0 and j == 0 else None)
                    with dve.If(t1 > t0 + MIN_TILES):
                        with dve.Fori(t0 + MIN_TILES, t1) as i:
                            step(i, e, par, None, None, None)
            tt = start_of(dve, E)
            finish_y(tt - 1, 1)

        @block.tensor
        def _(pe):
            def weights(par, part, first, n):
                return W[:, par, part, first:first + n]

            def rows_times(ps, par, offset, done):
                for k in range(KH):
                    for n, (a, c) in enumerate(PASSES):
                        op = pe.matmul(ps[:], xT[:, a, k, :], weights(par, c, offset + k * I, I),
                                       start=k == 0 and n == 0, stop=k == KH - 1 and n == 2)
                op.then_inc(done, 1)

            def transpose_rows():
                for n in range(2 * KH):
                    op = pe.transpose(psX[:, n * P:(n + 1) * P], xg[:, n * P:(n + 1) * P], ident16[:])
                op.then_inc(s_X, 1)

            def transpose_act(i):
                pe.wait_ge(s_ahi, i + 1)
                pe.wait_ge(s_alo, i + 1)
                for n in range(2 * KI):
                    op = pe.transpose(psA[:, n * P:(n + 1) * P], ahl[:, n // KI, n % KI * P:(n % KI + 1) * P], ident16[:])
                op.then_inc(s_A, 1)

            def down(i, par):
                pe.wait_ge(s_aTev, i + 1)
                pe.wait_ge(s_y0, i + 1)
                for h in range(2):
                    for k in range(KI):
                        for n, (a, c) in enumerate(PASSES):
                            op = pe.matmul(psY[:, h * HALF:(h + 1) * HALF], aT[:, a, k, :],
                                           weights(par, c, 2 * KH * I + k * H + h * HALF, HALF),
                                           start=k == 0 and n == 0, stop=k == KI - 1 and n == 2)
                op.then_inc(s_Y, 1)

            def step(i, e, par, first, prev_guard):
                def guarded(body):
                    if prev_guard is None:
                        body()
                    else:
                        with pe.If(prev_guard):
                            body()

                def weights_cut(chunks):
                    if first:
                        alone(pe, s_wlo, NCHUNK * e + chunks, s_past)

                pe.wait_ge(s_xTev, i + 1)
                weights_cut(PER_W)
                guarded(lambda: pe.wait_ge(s_gread, i))
                rows_times(psG, par, 0, s_G)

                def between():
                    transpose_act(i - 1)
                    pe.wait_ge(s_uread, i)
                guarded(between)
                weights_cut(2 * PER_W)
                rows_times(psU, par, KH * I, s_U)
                pe.wait_ge(s_xg, 16 * i + 32)
                transpose_rows()
                guarded(lambda: down(i - 1, 1 - par if first else par))
                weights_cut(3 * PER_W)

            pe.wait_ge(s_xg, 16)
            transpose_rows()
            with pe.Fori(0, PAIRS) as pair:
                for par in range(2):
                    e = pair * 2 + par
                    t0, t1 = start_of(pe, e), start_of(pe, e + 1)
                    step(t0, e, par, True, pair > 0 if par == 0 else None)
                    with pe.Fori(t0 + 1, t1) as i:
                        step(i, e, par, False, None)
            tt = start_of(pe, E)
            transpose_act(tt - 1)
            down(tt - 1, 1)


_INS = ["x", "ctx_1024", "L0_xattn_Wq", "L0_xattn_bq", "L0_xattn_Wk", "L0_xattn_bk", "L0_ffn_gate_w", "L0_ffn_gate_b",
        "L0_ffn_w_gate", "L0_ffn_b_gate", "L0_ffn_w_up", "L0_ffn_b_up", "L0_ffn_w_down", "L0_ffn_b_down"]


def kernel(**inputs):
    import numpy as _np
    import concourse.bacc as _bacc
    from concourse import mybir as _mybir
    from concourse.bass_utils import run_bass_kernel_spmd as _run

    nc = _bacc.Bacc("TRN2", target_bir_lowering=False, num_devices=1)
    arrays, args = {}, []
    for name in _INS:
        a = _np.ascontiguousarray(inputs[name])
        arrays[f"in_{name}"] = a
        args.append(nc.dram_tensor(f"in_{name}", a.shape, _mybir.dt.from_np(a.dtype), kind="ExternalInput").ap())
    b, l, h = inputs["x"].shape
    args.append(nc.dram_tensor("acc", (b * l + P, h), _mybir.dt.float32, kind="ExternalOutput").ap())
    xattn_moe_kernel(nc, *args)
    r = _run(nc, [arrays], core_ids=[0])
    return r.results[0]["acc"][0:b * l].reshape(b, l, h)
```

```python
from contextlib import ExitStack

import concourse.bass as bass
from concourse import mybir

ALU = mybir.AluOpType
ACT = mybir.ActivationFunctionType
AX_X = mybir.AxisListType.X
F32 = mybir.dt.float32
F16 = mybir.dt.float16
I32 = mybir.dt.int32
U32 = mybir.dt.uint32

P = 128
EPS = 1e-5
ALPHA = 1.702
LIMIT = 7.0
TOPK = 4
LO, HI = 0, 1
PASSES = ((HI, HI), (HI, LO), (LO, HI))
S_ROWS = 256.0
S_PROB = 16384.0
S_W = 256.0
S_ACT = 256.0
CHUNK = 2048
MIN_TILES = 3


class Tally:

    def __init__(self, sem, base=0):
        self.sem, self.base, self.n = sem, base, 0

    def inc(self, instruction, by=1):
        instruction.then_inc(self.sem, by)
        self.n += by

    def now(self):
        return self.base + self.n


def alone(eng, sem, value, passed):
    eng.wait_ge(sem, value)
    eng.sem_inc(passed, 1)


def at(nc, value, most):
    if isinstance(value, int):
        return bass.ds(value, 1)
    return bass.ds(nc.s_assert_within(value, 0, most, skip_runtime_bounds_check_because="guarded by the loops"), 1)


def xattn_moe_kernel(nc, x, ctx_in, Wq, bq, Wk, bk, gate_w, gate_b, w_gate, b_gate, w_up, b_up,
                     w_down, b_down, acc):
    B, L, H = x.shape
    C = ctx_in.shape[2]
    D = Wq.shape[0]
    E, _, I = w_gate.shape
    T = B * L
    NT = L // P
    KH, KC, KI = H // P, C // P, I // P
    HALF = 512
    assert L == H == 1024 and D == P and acc.shape[0] == T + P
    SLOTS = E * T
    NCHUNK = 3 * KH * I // CHUNK
    MAXT = 256
    assert T * TOPK // P + E * MIN_TILES <= MAXT - 4

    x_rows = x.rearrange("b (t p) h -> b t p h", p=P)
    acc_rows = acc.rearrange("(n p) h -> n p h", p=P)
    xn_tab = nc.dram_tensor("xn_tab", (T + P, 2 * H), F16, kind="Internal").ap()
    xn_rows = xn_tab.rearrange("(n p) h -> n p h", p=P)
    slots = nc.dram_tensor("slots", (SLOTS + 2 * P, 4), I32, kind="Internal").ap()

    with ExitStack() as whole:
        ident = whole.enter_context(nc.sbuf_tensor("ident", [P, P], F32))
        tile_start = whole.enter_context(nc.sbuf_tensor("tile_start", [1, 64], I32))
        slot_row = whole.enter_context(nc.sbuf_tensor("slot_row", [1, MAXT], I32))
        attention_and_routing(nc, locals())
        experts(nc, locals())


def attention_and_routing(nc, g):
    B, L, H, C, D, E, T = g["B"], g["L"], g["H"], g["C"], g["D"], g["E"], g["T"]
    NT, KH, KC, HALF, SLOTS, MAXT = g["NT"], g["KH"], g["KC"], g["HALF"], g["SLOTS"], g["MAXT"]
    x_rows, acc_rows, xn_rows, slots = g["x_rows"], g["acc_rows"], g["xn_rows"], g["slots"]
    ident, tile_start, slot_row = g["ident"], g["tile_start"], g["slot_row"]
    ctx_in, acc, xn_tab = g["ctx_in"], g["acc"], g["xn_tab"]

    with ExitStack() as ctx:
        def sb(name, shape, dt):
            return ctx.enter_context(nc.sbuf_tensor(name, shape, dt))

        def psum(name, shape, dt):
            return ctx.enter_context(nc.psum_tensor(name, shape, dt))

        def sem(name):
            return ctx.enter_context(nc.semaphore(name))

        x1 = sb("x1", [P, 2, H], F32)
        xr = sb("xr", [P, 2, H], F32)
        cx = sb("cx", [P, NT, C], F32)
        cxT = sb("cxT", [P, KC, L], F32)
        qk = sb("qk", [P, 2, L], F32)
        XT = sb("XT", [P, KH, L, 2], F16)
        AT = sb("AT", [P, 2, 2, KH, L], F16)
        xs = sb("xs", [P, H], F32)
        xnh = sb("xnh", [P, H, 2], F16)
        prob = sb("prob", [P, L], F32)
        ah = sb("ah", [P, 2, L, 2], F16)
        xs2 = sb("xs2", [P, H], F32)
        x2h = sb("x2h", [P, 2, H, 2], F16)
        x2T = sb("x2T", [P, KH, P], F32)
        before = sb("before", [P, P], F32)
        upto = sb("upto", [E, E], F32)
        ones = sb("ones", [P, P], F32)
        WT = sb("WT", [P, 2, KC, D], F32)
        gateT = sb("gateT", [P, KH, E], F32)
        bqk = sb("bqk", [P, 2], F32)
        gb = sb("gb", [P, E], F32)
        iota_i = sb("iota_i", [P, E], I32)
        iota_e = sb("iota_e", [P, E], F32)
        ebase = sb("ebase", [P, E], F32)
        tok = sb("tok", [P, 1], F32)
        tok_i = sb("tok_i", [P, 1], I32)
        st = sb("st", [P, 2, 6], F32)
        mv = sb("mv", [P, 2], F32)
        ve = sb("ve", [P, 2], F32)
        neg_half = sb("neg_half", [P, 1], F32)
        rstd = sb("rstd", [P, 2], F32)
        mx = sb("mx", [P, 2], F32)
        nmx = sb("nmx", [P, 2], F32)
        psm = sb("psm", [P, 2], F32)
        sc = sb("sc", [P, 2], F32)
        lg = sb("lg", [P, E], F32)
        v8 = sb("v8", [P, 2, 8], F32)
        i8 = sb("i8", [P, 8], U32)
        i4 = sb("i4", [P, TOPK], F32)
        nv0 = sb("nv0", [P, 2], F32)
        oh = sb("oh", [P, 2, TOPK, E], F32)
        mask = sb("mask", [P, 2, E], F32)
        seen = sb("seen", [P, E], F32)
        rk = sb("rk", [P, E], F32)
        junk = sb("junk", [P, TOPK, E], F32)
        dest_f = sb("dest_f", [P, TOPK], F32)
        dest = sb("dest", [P, 2, TOPK], U32)
        ex = sb("ex", [P, 2, TOPK], F32)
        es = sb("es", [P, 2], F32)
        er = sb("er", [P, 1], F32)
        wt = sb("wt", [P, TOPK], F32)
        pack = sb("pack", [P, 2, TOPK, 4], I32)
        ncol = sb("ncol", [E, 4], F32)
        ge = sb("ge", [E, MAXT], F32)
        iota_t = sb("iota_t", [E, MAXT], F32)
        iota_ti = sb("iota_ti", [E, MAXT], I32)
        rowf = sb("rowf", [1, MAXT], F32)
        padding = ah[:, :, :, :].rearrange("p a b c -> p (a b c)").bitcast(I32).rearrange("p (r c) -> p r c", c=4)
        wqk_in = xs[:, :].rearrange("p (w c) -> p w c", w=2)
        gate_in = prob[0:E, :]
        xnh_w = xnh[:, :, :].rearrange("p h a -> p (h a)").bitcast(F32)
        ah_w = [ah[:, j, :, :].rearrange("p h a -> p (h a)").bitcast(F32) for j in range(2)]
        XT_w = XT[:, :, :, :].rearrange("p k l a -> p (k l a)").bitcast(F32).rearrange("p (k l) -> p k l", k=KH)

        psE = psum("psE", [P, 2 * HALF], F32)
        psM = psum("psM", [P, 2 * HALF], F32)
        psT = psum("psT", [P, 2 * HALF], F32)
        psQ = psum("psQ", [P, HALF], F32)
        psR = psum("psR", [P, HALF], F32)
        psT_pairs = psT[:, :].bitcast(F16).rearrange("p (k q a) -> p a k q", k=KH, a=2)
        quarter = [psM[:, 0:HALF], psM[:, HALF:], psE[:, 0:HALF], psE[:, HALF:]]

        s_x1 = [sem(f"x1_in{t}") for t in range(2)]
        s_xr = [sem(f"xr_in{t}") for t in range(2)]
        s_ctx = sem("ctx_in")
        s_past = sem("waits_passed")
        s_small = sem("small_in")
        s_const = sem("consts")
        s_padfill = sem("pad_filled")
        s_padout = sem("pad_stored")
        s_ready = sem("dve_consts")
        s_wT = sem("w_transposed")
        s_wTev = sem("w_evacuated")
        s_x2out = [sem(f"x2_out{t}") for t in range(2)]
        s_xnout = [sem(f"xn_out{t}") for t in range(2)]
        s_slotout = [sem(f"slot_out{t}") for t in range(2)]
        s_cT = sem("ctx_transposed")
        s_cTev = sem("ctxT_evacuated")
        s_qk = sem("qk_done")
        s_qkev = sem("qk_evacuated")
        s_E = sem("energy_done")
        s_nmx = sem("negmax_ready")
        s_exp = sem("exp_done")
        s_sc = sem("prob_scale_ready")
        s_ahi = sem("prob_hi")
        s_alo = sem("prob_lo")
        s_AT = sem("prob_transposed")
        s_ATev = sem("probT_evacuated")
        s_var = [sem(f"variance{n}_ready") for n in (1, 2)]
        s_rstd = [sem(f"rstd{n}_ready") for n in (1, 2)]
        s_xs = sem("ln1_ready")
        s_xhi = sem("ln1_hi")
        s_xlo = sem("ln1_lo")
        s_xT = sem("ln1_transposed")
        s_xTev = sem("ln1T_evacuated")
        s_xm = sem("xm_done")
        s_x2 = sem("x2_ready")
        s_xs2 = sem("ln2_ready")
        s_hi2 = sem("ln2_hi")
        s_lo2 = sem("ln2_lo")
        s_x2T = sem("ln2_transposed")
        s_x2Tev = sem("ln2T_evacuated")
        s_lgt = sem("logits_done")
        s_lgev = sem("logits_read")
        s_nv0 = sem("top1_ready")
        s_ex = sem("weights_exp")
        s_mask = sem("mask_ready")
        s_rank = sem("rank_done")
        s_seen = sem("seen_ready")
        s_pack = sem("pack_ready")
        s_ln = [sem(f"ln{n}_chain") for n in (1, 2)]
        s_soft = sem("softmax_chain")
        s_top = sem("topk_chain")
        s_slot = sem("slot_chain")
        s_once = sem("dve_once")
        s_tail = sem("tail_pe")
        s_tailv = sem("tail_dve")
        block = ctx.enter_context(nc.Block())

        ALL = NT + 4

        def par(b):
            return slice(b % 2, b % 2 + 1) if isinstance(b, int) else at(nc, b % 2, 1)

        def schedule(eng, step, prepare):
            prepare(0, 0)
            prepare(0, 1)
            for s in range(NT + 1):
                step(s, 0, None)
            prepare(1, 0)
            prepare(1, 1)
            with eng.Fori(0, B - 1) as b:
                for s in range(NT + 1):
                    step(s, b + 1, b)
                with eng.If(b < B - 2):
                    prepare(b + 2, 0)
                step(NT + 1, None, b)
                with eng.If(b < B - 2):
                    prepare(b + 2, 1)
                for s in range(NT + 2, ALL):
                    step(s, None, b)
            for s in range(ALL):
                step(s, None, B - 1)

        @block.sync
        def _(sp):
            for t in range(2):
                sp.sem_inc(s_xnout[t], 16)

            def load_x(dst, sems, b, t):
                sp.dma_start(dst[:, t % 2, :], x_rows[at(nc, b, B - 1), t].rearrange("o p h -> (o p) h")).then_inc(sems[t % 2], 16)

            def load_ctx(b):
                sp.dma_start(cx[:], ctx_in[at(nc, b, B - 1)].rearrange("o (t p) c -> p (o t) c", p=P)).then_inc(s_ctx, 16)

            sp.dma_start(wqk_in[:, 0, :], g["Wq"]).then_inc(s_small, 16)
            sp.dma_start(wqk_in[:, 1, :], g["Wk"]).then_inc(s_small, 16)
            sp.dma_start(gate_in, g["gate_w"]).then_inc(s_small, 16)
            sp.dma_start(bqk[:, 0:1], g["bq"].rearrange("(d o) -> d o", o=1)).then_inc(s_small, 16)
            sp.dma_start(bqk[:, 1:2], g["bk"].rearrange("(d o) -> d o", o=1)).then_inc(s_small, 16)
            sp.dma_start(gb[:], g["gate_b"].rearrange("(o e) -> o e", o=1).to_broadcast([P, E])).then_inc(s_small, 16)
            load_ctx(0)
            for t in range(2):
                load_x(x1, s_x1, 0, t)
            sp.wait_ge(s_padfill, 2)
            half = SLOTS // P // 2
            for part in range(2):
                sp.dma_start(slots[0:SLOTS, :].rearrange("(p r) c -> p r c", p=P)[:, part * half:(part + 1) * half, :],
                             padding).then_inc(s_padout, 16)
            sp.dma_start(slots[SLOTS:SLOTS + 2 * P, :].rearrange("(o r) c -> o r c", o=1),
                         padding[0:1, 0:2 * P, :]).then_inc(s_padout, 16)
            zero = x2T[:, :, :].rearrange("p k q -> p (k q)")
            sp.dma_start(xn_rows[T // P], zero.bitcast(F16)).then_inc(s_padout, 16)
            sp.dma_start(acc_rows[T // P], zero).then_inc(s_padout, 16)
            for t in range(2):
                load_x(xr, s_xr, 0, t)

            def prepare(b, part):
                if part == 1:
                    def context():
                        sp.wait_ge(s_cT, b * NT + NT)
                        load_ctx(b + 1)
                    if isinstance(b, int):
                        context()
                    else:
                        with sp.If(b < B - 1):
                            context()
                    sp.wait_ge(s_xs, b * NT + 1)
                    load_x(x1, s_x1, b, 2)

            def step(s, b1, b2):
                if b1 is not None and s < NT - 1:
                    def more():
                        sp.wait_ge(s_xs, b1 * NT + s + 2)
                        if s + 3 < NT:
                            load_x(x1, s_x1, b1, s + 3)
                        else:
                            load_x(x1, s_x1, b1 + 1, s + 3 - NT)
                    if s + 3 < NT or isinstance(b1, int):
                        more()
                    elif s + 3 - NT < 2:
                        with sp.If(b1 < B - 1):
                            more()
                if b2 is not None and s < NT:
                    n = b2 * NT + s
                    sp.wait_ge(s_x2, n + 1)
                    sp.dma_start(acc_rows[bass.ds(n, 1)].rearrange("o p h -> (o p) h"), xr[:, s % 2, :]).then_inc(s_x2out[s % 2], 16)
                    sp.wait_ge(s_lo2, n + 1)
                    sp.dma_start(xn_rows[bass.ds(n, 1)].rearrange("o p h -> (o p) h"),
                                 x2h[:, s % 2].rearrange("p h a -> p (h a)")).then_inc(s_xnout[s % 2], 16)

                    def reload():
                        alone(sp, s_x2out[s % 2], 16 * (b2 * (NT // 2) + s // 2 + 1), s_past)
                        load_x(xr, s_xr, b2 if s < NT - 2 else b2 + 1, (s + 2) % NT)
                    if s < NT - 2:
                        reload()
                    elif not isinstance(b2, int):
                        reload()

            schedule(sp, step, prepare)
            for t in range(2):
                sp.wait_ge(s_x2out[t], 16 * B * NT // 2)
            for t in range(2):
                sp.wait_ge(s_xnout[t], 16 * (B * NT // 2 + 1))

        @block.gpsimd
        def _(pool):
            pool.memset(ident[:], 0.0).then_inc(s_const, 1)
            pool.memset(ones[:], 1.0).then_inc(s_const, 1)
            pool.memset(before[:], 1.0).then_inc(s_const, 1)
            pool.memset(upto[:], 1.0).then_inc(s_const, 1)
            pool.memset(seen[:], 0.0).then_inc(s_const, 1)
            pool.wait_ge(s_const, 5)
            pool.affine_select(out=ident[:], in_=ident[:], compare_op=ALU.not_equal, fill=1.0, base=0,
                               pattern=[[-1, P]], channel_multiplier=1).then_inc(s_const, 1)
            pool.affine_select(out=before[:], in_=before[:], compare_op=ALU.is_gt, fill=0.0, base=0,
                               pattern=[[1, P]], channel_multiplier=-1).then_inc(s_const, 1)
            pool.affine_select(out=upto[:], in_=upto[:], compare_op=ALU.is_ge, fill=0.0, base=0,
                               pattern=[[1, E]], channel_multiplier=-1).then_inc(s_const, 1)
            pool.iota(iota_i[:], pattern=[[1, E]], base=0, channel_multiplier=0).then_inc(s_const, 1)
            pool.iota(iota_ti[:], pattern=[[1, MAXT]], base=0, channel_multiplier=0).then_inc(s_const, 1)
            pool.iota(tok_i[:], pattern=[[0, 1]], base=0, channel_multiplier=1).then_inc(s_const, 1)
            pool.memset(padding, 0).then_inc(s_const, 1)
            pool.memset(x2T[:], 0.0).then_inc(s_padfill, 1)
            pool.memset(neg_half[:], -0.5).then_inc(s_const, 1)
            pool.memset(pack[:], 0).then_inc(s_const, 1)
            pool.wait_ge(s_const, 14)
            pool.iota(padding[:, :, 0].rearrange("p (a l) -> p a l", l=P), pattern=[[0, padding.shape[1] // P], [1, P]],
                      base=T, channel_multiplier=0).then_inc(s_padfill, 1)
            pool.wait_ge(s_padout, 16 * 5)

            def inverse_root(which, nth):
                pool.wait_ge(s_var[which], nth)
                pool.tensor_tensor(out=rstd[:, which:which + 1], in0=ve[:, which:which + 1], in1=neg_half[:],
                                   op=ALU.pow).then_inc(s_rstd[which], 1)

            def prepare(b, part):
                if part == 0:
                    inverse_root(0, b * NT + 1)

            def step(s, b1, b2):
                if b1 is not None and s < NT - 1:
                    inverse_root(0, b1 * NT + s + 2)
                if b2 is not None and s >= 4:
                    n = s - 4
                    alone(pool, s_pack, b2 * NT + n + 1, s_past)
                    for k in range(TOPK):
                        pool.indirect_dma_start(
                            out=slots[:, :], out_offset=bass.IndirectOffsetOnAxis(dest[:, n % 2, k:k + 1], 0),
                            in_=pack[:, n % 2, k, :], in_offset=None).then_inc(s_slotout[n % 2], 16)
                if b2 is not None and s < NT:
                    inverse_root(1, b2 * NT + s + 1)

            schedule(pool, step, prepare)
            for t in range(2):
                pool.wait_ge(s_slotout[t], 16 * TOPK * (B * NT // 2))

        @block.scalar
        def _(act):
            for n in range(2 * KC + KH):
                act.wait_ge(s_wT, n + 1)
                if n < 2 * KC:
                    act.activation(WT[:, n // KC, n % KC, :], psT[:, n % 2 * HALF:n % 2 * HALF + D], ACT.Copy).then_inc(s_wTev, 1)
                else:
                    act.activation(gateT[:, n - 2 * KC, :], psT[:, n % 2 * HALF:n % 2 * HALF + E], ACT.Copy).then_inc(s_wTev, 1)
            act.wait_ge(s_padout, 16 * 5)

            def prepare(b, part):
                if part == 0:
                    for t in range(NT):
                        act.wait_ge(s_cT, b * NT + t + 1)
                        act.activation(cxT[:, :, t * P:(t + 1) * P],
                                       psT[:, t % 2 * HALF:(t % 2 + 1) * HALF].rearrange("p (c q) -> p c q", c=KC),
                                       ACT.Copy).then_inc(s_cTev, 1)
                    act.wait_ge(s_xs, b * NT + 1)
                    act.activation(xnh[:, :, HI], xs[:], ACT.Copy, scale=S_ROWS).then_inc(s_xhi, 1)

            def step(s, b1, b2):
                if b1 is not None:
                    t1, m = b1 * NT, s
                    if m < NT:
                        act.wait_ge(s_nmx, t1 + m + 1)
                        act.activation(prob[:], psE[:], ACT.Exp, bias=nmx[:, 0:1], accum_out=psm[:, 0:1]).then_inc(s_exp, 1)
                        act.wait_ge(s_sc, t1 + m + 1)
                        act.activation(ah[:, m % 2, :, HI], prob[:], ACT.Copy, scale=sc[:, 0:1]).then_inc(s_ahi, 1)
                        act.wait_ge(s_xT, t1 + m + 1)
                        act.activation(XT_w[:, :, m * P:(m + 1) * P], psT[:, :].rearrange("p (k q) -> p k q", q=P),
                                       ACT.Copy).then_inc(s_xTev, 1)
                    if m < NT - 1:
                        act.wait_ge(s_xs, t1 + m + 2)
                        act.activation(xnh[:, :, HI], xs[:], ACT.Copy, scale=S_ROWS).then_inc(s_xhi, 1)
                    if m >= 1:
                        act.wait_ge(s_AT, t1 + m)
                        dst = AT[:, par(b1), :, :, (m - 1) * P:m * P].rearrange("p o a k q -> p (o a) k q")
                        act.activation(dst, psT_pairs, ACT.Copy).then_inc(s_ATev, 1)
                if b2 is not None:
                    t2, t = b2 * NT, s
                    if 3 <= t < NT + 3:
                        n = t - 3
                        act.wait_ge(s_nv0, t2 + n + 1)
                        act.activation(ex[:, n % 2, :], v8[:, n % 2, 0:TOPK], ACT.Exp, bias=nv0[:, n % 2:n % 2 + 1],
                                       accum_out=es[:, n % 2:n % 2 + 1]).then_inc(s_ex, 1)
                    if 1 <= t <= NT:
                        act.wait_ge(s_x2T, t2 + t)
                        act.activation(x2T[:], psT[:, :].rearrange("p (k q) -> p k q", q=P), ACT.Copy).then_inc(s_x2Tev, 1)
                    if t < NT:
                        act.wait_ge(s_xnout[t % 2], 16 * (b2 * (NT // 2) + t // 2 + 1))
                        act.wait_ge(s_xs2, t2 + t + 1)
                        act.activation(x2h[:, t % 2, :, HI], xs2[:], ACT.Copy, scale=S_ROWS).then_inc(s_hi2, 1)

            schedule(act, step, prepare)

        @block.tensor
        def _(pe):
            pe.wait_ge(s_const, 8)
            pe.wait_ge(s_small, 16 * 6)
            for n in range(2 * KC + KH):
                if n >= 2:
                    pe.wait_ge(s_wTev, n - 1)
                dst = psT[:, n % 2 * HALF:]
                if n < 2 * KC:
                    pe.transpose(dst[:, 0:D], wqk_in[:, n // KC, n % KC * P:(n % KC + 1) * P], ident[:]).then_inc(s_wT, 1)
                else:
                    k = n - 2 * KC
                    pe.transpose(dst[:, 0:E], gate_in[:, k * P:(k + 1) * P], ident[0:E, 0:E]).then_inc(s_wT, 1)
            pe.wait_ge(s_wTev, 2 * KC + KH)
            pe.wait_ge(s_ready, 1)

            def energies(b, m):
                for h in range(2):
                    op = pe.matmul(psE[:, h * HALF:(h + 1) * HALF], qk[:, 0, m * P:(m + 1) * P],
                                   qk[:, 1, h * HALF:(h + 1) * HALF], start=True, stop=True)
                op.then_inc(s_E, 1)

            def transpose_words(src, done):
                for k in range(KH):
                    op = pe.transpose(psT[:, k * P:(k + 1) * P], src[:, k * P:(k + 1) * P], ident[:])
                op.then_inc(done, 1)

            def prepare(b, part):
                t1 = b * NT
                if part == 0:
                    pe.wait_ge(s_ctx, 16 * b + 16)
                    if not isinstance(b, int):
                        pe.wait_ge(s_x2Tev, t1 - NT)
                    if not isinstance(b, int) or b > 0:
                        pe.wait_ge(s_ATev, t1)
                    for t in range(NT):
                        if t >= 2:
                            pe.wait_ge(s_cTev, t1 + t - 1)
                        for c in range(KC):
                            op = pe.transpose(psT[:, t % 2 * HALF + c * P:t % 2 * HALF + (c + 1) * P],
                                              cx[:, t, c * P:(c + 1) * P], ident[:])
                        op.then_inc(s_cT, 1)
                else:
                    pe.wait_ge(s_cTev, t1 + NT)
                    for n in range(4):
                        for c in range(KC):
                            op = pe.matmul(quarter[n], WT[:, n // 2, c, :], cxT[:, c, n % 2 * HALF:(n % 2 + 1) * HALF],
                                           start=c == 0, stop=c == KC - 1)
                        op.then_inc(s_qk, 1)
                    pe.wait_ge(s_qkev, b * 4 + 4)
                    energies(b, 0)

            def half_product(b2, t, h):
                for k in range(KH):
                    for n, (a, c) in enumerate(PASSES):
                        op = pe.matmul(psM[:, h * HALF:(h + 1) * HALF], XT[:, k, t * P:(t + 1) * P, a],
                                       AT[:, par(b2), c, k, h * HALF:(h + 1) * HALF].rearrange("p o q -> p (o q)"),
                                       start=k == 0 and n == 0, stop=k == KH - 1 and n == 2)
                return op

            def step(s, b1, b2):
                t1 = None if b1 is None else b1 * NT
                t2 = None if b2 is None else b2 * NT
                if b2 is not None and s < NT:
                    if s == 0:
                        pe.wait_ge(s_ATev, t2 + NT)
                        pe.wait_ge(s_xTev, t2 + NT)
                    else:
                        pe.wait_ge(s_x2, t2 + s)
                    half_product(b2, s, 0)
                    half_product(b2, s, 1).then_inc(s_xm, 1)
                if b1 is not None and s < NT:
                    pe.wait_ge(s_xlo, t1 + s + 1)
                    if b2 is not None and s >= 2:
                        pe.wait_ge(s_x2Tev, t2 + s - 1)
                    if s >= 2:
                        pe.wait_ge(s_ATev, t1 + s - 1)
                    elif s == 1:
                        pe.wait_ge(s_xTev, t1 + 1)
                    transpose_words(xnh_w, s_xT)
                if b1 is not None and s < NT - 1:
                    pe.wait_ge(s_exp, t1 + s + 1)
                    energies(b1, s + 1)
                if b1 is not None and s >= 1:
                    pe.wait_ge(s_alo, t1 + s)
                    if s < NT:
                        pe.wait_ge(s_xTev, t1 + s + 1)
                    else:
                        pe.wait_ge(s_ATev, t1 + s - 1)
                        if b2 is not None:
                            pe.wait_ge(s_x2Tev, t2 + s - 1)
                    transpose_words(ah_w[(s - 1) % 2], s_AT)
                if b2 is not None and s >= 3 and s < NT + 3:
                    n = s - 3
                    pe.wait_ge(s_mask, t2 + n + 1)
                    pe.wait_ge(s_seen, t2 + n + 1)
                    pe.matmul(psQ[:, 0:E], before[:], mask[:, n % 2, :], start=True, stop=False)
                    pe.matmul(psQ[:, 0:E], ones[:], seen[:], start=False, stop=True).then_inc(s_rank, 1)
                if b2 is not None and 2 <= s < NT + 2:
                    n = s - 2
                    pe.wait_ge(s_x2Tev, t2 + n + 1)
                    if n >= 1:
                        pe.wait_ge(s_lgev, t2 + n)
                    for k in range(KH):
                        op = pe.matmul(psR[:, 0:E], x2T[:, k, :], gateT[:, k, :], start=k == 0, stop=k == KH - 1)
                    op.then_inc(s_lgt, 1)
                if b2 is not None and 1 <= s < NT + 1:
                    pe.wait_ge(s_xs2, t2 + s)
                    if b1 is not None:
                        pe.wait_ge(s_ATev, t1 + s)
                    transpose_words(xs2, s_x2T)

            schedule(pe, step, prepare)
            pe.wait_ge(s_seen, B * NT + 1)
            pe.matmul(psQ[0:E, 0:1], seen[:], ones[:, 0:1], start=True, stop=True).then_inc(s_tail, 1)
            pe.wait_ge(s_tailv, 1)
            pe.matmul(psR[0:E, 0:1], upto[:], ncol[:, 0:1], start=True, stop=True).then_inc(s_tail, 1)
            pe.wait_ge(s_tailv, 2)
            pe.matmul(psE[0:1, 0:E], ncol[:, 0:1], upto[:], start=True, stop=True).then_inc(s_tail, 1)
            pe.matmul(psM[0:1, 0:MAXT], ones[0:E, 0:1], ge[:], start=True, stop=True).then_inc(s_tail, 1)

        @block.vector
        def _(dve):
            def link(tally, ins):
                tally.inc(ins)
                dve.wait_ge(tally.sem, tally.now())

            def layernorm(which, out, src, ready, n):
                v = Tally(s_ln[which], n * 3)
                for h in range(2):
                    v.inc(dve.bn_stats(st[:, h, :], src[:, h * HALF:(h + 1) * HALF]))
                alone(dve, v.sem, v.now(), s_past)
                link(v, dve.bn_aggr(mv[:], st[:, :, :]))
                dve.tensor_scalar(ve[:, which:which + 1], mv[:, 1:2], EPS, None, ALU.add).then_inc(s_var[which], 1)
                dve.wait_ge(s_rstd[which], n + 1)
                dve.tensor_scalar(out, src, mv[:, 0:1], rstd[:, which:which + 1], ALU.subtract, ALU.mult).then_inc(ready, 1)

            def split_rows(b, m):
                dve.wait_ge(s_xhi, b * NT + m + 1)
                dve.scalar_tensor_tensor(out=xnh[:, :, LO], in0=xs[:], scalar=S_ROWS, in1=xnh[:, :, HI],
                                         op0=ALU.mult, op1=ALU.subtract).then_inc(s_xlo, 1)

            def normalize(b, m):
                dve.wait_ge(s_x1[m % 2], 16 * (b * (NT // 2) + m // 2 + 1))
                layernorm(0, xs[:], x1[:, m % 2, :], s_xs, b * NT + m)

            first = Tally(s_once)
            dve.wait_ge(s_const, 11)
            link(first, dve.tensor_copy(iota_e[:], iota_i[:]))
            link(first, dve.tensor_scalar(ebase[:], iota_e[:], float(T), None, ALU.mult))
            link(first, dve.tensor_copy(iota_t[:], iota_ti[:]))
            link(first, dve.tensor_copy(tok[:], tok_i[:]))
            dve.memset(lg[:], 0.0).then_inc(s_ready, 1)
            dve.memset(psm[:], 0.0).then_inc(s_seen, 1)
            dve.wait_ge(s_small, 16 * 6)
            dve.wait_ge(s_wTev, 2 * KC + KH)

            def prepare(b, part):
                if part == 0:
                    normalize(b, 0)
                else:
                    for n in range(4):
                        dve.wait_ge(s_qk, b * 4 + n + 1)
                        dve.tensor_scalar(qk[:, n // 2, n % 2 * HALF:(n % 2 + 1) * HALF], quarter[n],
                                          bqk[:, n // 2:n // 2 + 1], None, ALU.add).then_inc(s_qkev, 1)
                    split_rows(b, 0)

            def step(s, b1, b2):
                t1 = None if b1 is None else b1 * NT
                t2 = None if b2 is None else b2 * NT
                if b1 is not None and s < NT:
                    v = Tally(s_soft, (t1 + s) * 2)
                    dve.wait_ge(s_E, t1 + s + 1)
                    link(v, dve.reduce_max(mx[:, 0:1], psE[:], axis=AX_X))
                    dve.tensor_scalar(nmx[:, 0:1], mx[:, 0:1], -1.0, None, ALU.mult).then_inc(s_nmx, 1)
                    if s < NT - 1:
                        normalize(b1, s + 1)
                    dve.wait_ge(s_exp, t1 + s + 1)
                    link(v, dve.reciprocal(sc[:, 1:2], psm[:, 0:1]))
                    dve.tensor_scalar(sc[:, 0:1], sc[:, 1:2], S_PROB, None, ALU.mult).then_inc(s_sc, 1)
                    assert v.n == 2
                if b2 is not None and 3 <= s < NT + 3:
                    n = s - 3
                    j = n % 2
                    v = Tally(s_top, (t2 + n) * 7)
                    dve.wait_ge(s_lgt, t2 + n + 1)
                    dve.tensor_tensor(lg[:], psR[:, 0:E], gb[:], ALU.add).then_inc(s_lgev, 1)
                    alone(dve, s_lgev, t2 + n + 1, s_past)
                    link(v, dve.max(v8[:, j, :], lg[:]))
                    dve.tensor_scalar(nv0[:, j:j + 1], v8[:, j, 0:1], -1.0, None, ALU.mult).then_inc(s_nv0, 1)
                    link(v, dve.max_index(i8[:], v8[:, j, :], lg[:]))
                    link(v, dve.tensor_copy(i4[:], i8[:, 0:TOPK]))
                    for k in range(TOPK):
                        v.inc(dve.tensor_scalar(oh[:, j, k, :], iota_e[:], i4[:, k:k + 1], None, ALU.is_equal))
                    dve.wait_ge(v.sem, v.now())
                    dve.tensor_reduce(mask[:, j, :], oh[:, j].rearrange("p k e -> p e k"), AX_X, ALU.add).then_inc(s_mask, 1)
                    assert v.n == 7
                if b2 is not None and s >= 4:
                    n = s - 4
                    j = n % 2
                    v = Tally(s_slot, (t2 + n) * 11)
                    dve.wait_ge(s_rank, t2 + n + 1)
                    link(v, dve.tensor_tensor(rk[:], psQ[:, 0:E], ebase[:], ALU.add))
                    for k in range(TOPK):
                        v.inc(dve.tensor_tensor_reduce(out=junk[:, k, :], in0=oh[:, j, k, :], in1=rk[:], scale=1.0, scalar=0.0,
                                                       op0=ALU.mult, op1=ALU.add, accum_out=dest_f[:, k:k + 1]))
                    alone(dve, v.sem, v.now(), s_past)
                    if n < 2 and not isinstance(b2, int):
                        with dve.If(b2 > 0):
                            alone(dve, s_slotout[j], 16 * TOPK * (NT // 2) * b2, s_past)
                    else:
                        dve.wait_ge(s_slotout[j], 16 * TOPK * (b2 * (NT // 2) + n // 2))
                    v.inc(dve.tensor_copy(dest[:, j, :], dest_f[:]))
                    dve.wait_ge(s_ex, t2 + n + 1)
                    link(v, dve.reciprocal(er[:], es[:, j:j + 1]))
                    link(v, dve.tensor_scalar(wt[:], ex[:, j, :], er[:], None, ALU.mult))
                    v.inc(dve.tensor_copy(pack[:, j, :, 1].bitcast(F32), wt[:]))
                    v.inc(dve.tensor_scalar(pack[:, j, :, 2].bitcast(F32), wt[:], 1.0 / (S_ACT * S_W), None, ALU.mult))
                    v.inc(dve.tensor_copy(pack[:, j, :, 0], tok[:].to_broadcast([P, TOPK])))
                    dve.wait_ge(v.sem, v.now())
                    dve.tensor_tensor(seen[:], seen[:], mask[:, j, :], ALU.add).then_inc(s_seen, 1)
                    dve.tensor_scalar(tok[:], tok[:], float(P), None, ALU.add).then_inc(s_pack, 1)
                    alone(dve, s_pack, t2 + n + 1, s_past)
                    assert v.n == 11
                if b1 is not None and s < NT:
                    dve.wait_ge(s_ahi, t1 + s + 1)
                    dve.wait_ge(s_sc, t1 + s + 1)
                    dve.scalar_tensor_tensor(out=ah[:, s % 2, :, LO], in0=prob[:], scalar=sc[:, 0:1],
                                             in1=ah[:, s % 2, :, HI], op0=ALU.mult, op1=ALU.subtract).then_inc(s_alo, 1)
                if b2 is not None and s < NT:
                    dve.wait_ge(s_xr[s % 2], 16 * (b2 * (NT // 2) + s // 2 + 1))
                    dve.wait_ge(s_xm, t2 + s + 1)
                    dve.scalar_tensor_tensor(out=xr[:, s % 2, :], in0=psM[:], scalar=1.0 / (S_ROWS * S_PROB),
                                             in1=xr[:, s % 2, :], op0=ALU.mult, op1=ALU.add).then_inc(s_x2, 1)
                    alone(dve, s_x2, t2 + s + 1, s_past)
                    if s >= 1:
                        alone(dve, s_x2T, t2 + s, s_past)
                    layernorm(1, xs2[:], xr[:, s % 2, :], s_xs2, t2 + s)
                if b1 is not None and s < NT - 1:
                    split_rows(b1, s + 1)
                if b2 is not None and s < NT:
                    dve.wait_ge(s_hi2, t2 + s + 1)
                    dve.scalar_tensor_tensor(out=x2h[:, s % 2, :, LO], in0=xs2[:], scalar=S_ROWS, in1=x2h[:, s % 2, :, HI],
                                             op0=ALU.mult, op1=ALU.subtract).then_inc(s_lo2, 1)

            schedule(dve, step, prepare)
            z = Tally(s_once, first.n)
            dve.wait_ge(s_tail, 1)
            link(z, dve.tensor_copy(ncol[:, 3:4], psQ[0:E, 0:1]))
            link(z, dve.tensor_scalar(ge[:, 0:T // P], iota_t[:, 0:T // P], float(P), ncol[:, 3:4], ALU.mult, ALU.is_lt))
            link(z, dve.reduce_sum(ncol[:, 2:3], ge[:, 0:T // P], axis=AX_X))
            dve.tensor_scalar(ncol[:, 0:1], ncol[:, 2:3], float(MIN_TILES), None, ALU.max).then_inc(s_tailv, 1)
            dve.wait_ge(s_tailv, 1)
            link(z, dve.tensor_scalar(ncol[:, 1:2], ncol[:, 0:1], -float(P), float(T), ALU.mult, ALU.add))
            dve.wait_ge(s_tail, 2)
            link(z, dve.tensor_copy(ncol[:, 2:3], psR[0:E, 0:1]))
            link(z, dve.tensor_scalar(ge[:], iota_t[:], ncol[:, 2:3], ncol[:, 1:2], ALU.is_ge, ALU.mult))
            dve.memset(tile_start[:], 0).then_inc(s_tailv, 1)
            dve.wait_ge(s_tailv, 2)
            dve.wait_ge(s_tail, 3)
            dve.tensor_copy(tile_start[0:1, 1:E + 1], psE[0:1, 0:E]).then_inc(s_tailv, 1)
            dve.wait_ge(s_tail, 4)
            link(z, dve.scalar_tensor_tensor(out=rowf[:], in0=iota_t[0:1, :], scalar=float(P), in1=psM[0:1, 0:MAXT],
                                             op0=ALU.mult, op1=ALU.add))
            dve.tensor_copy(slot_row[:], rowf[:]).then_inc(s_tailv, 1)
            dve.wait_ge(s_tailv, 4)


def experts(nc, g):
    H, E, I, T = g["H"], g["E"], g["I"], g["T"]
    KH, KI, HALF, NCHUNK, MAXT = g["KH"], g["KI"], g["HALF"], g["NCHUNK"], g["MAXT"]
    slots, xn_tab, acc = g["slots"], g["xn_tab"], g["acc"]
    ident, tile_start, slot_row = g["ident"], g["tile_start"], g["slot_row"]
    w_dram = [g["w_gate"].rearrange("e (k p) n -> e p k n", p=P), g["w_up"].rearrange("e (k p) n -> e p k n", p=P),
              g["w_down"].rearrange("e (k p) n -> e p k n", p=P)]
    RING = 3
    PAIRS = E // 2
    PER_W = NCHUNK // 3
    CUT = [[0, 1], [2, 3], [4, 5]]
    LOAD = [[3, 4], [5], [6, 7, 8]]
    assert NCHUNK == 6 and len(CUT) == MIN_TILES

    with ExitStack() as ctx:
        def sb(name, shape, dt):
            return ctx.enter_context(nc.sbuf_tensor(name, shape, dt))

        def psum(name, shape, dt):
            return ctx.enter_context(nc.psum_tensor(name, shape, dt))

        def sem(name):
            return ctx.enter_context(nc.semaphore(name))

        W = sb("W", [P, 2, 2, NCHUNK * CHUNK], F16)
        stage = sb("stage", [P, RING, CHUNK], F32)
        bias = sb("bias", [P, 2, 2 * I + H], F32)
        idxg = sb("idxg", [P, 4], I32)
        idxs = sb("idxs", [P, 4], I32)
        xg = sb("xg", [P, 2 * H], F16)
        xT = sb("xT", [P, KH, P, 2], F16)
        gt = sb("gt", [P, I], F32)
        sg = sb("sg", [P, I], F32)
        up = sb("up", [P, I], F32)
        av = sb("av", [P, I], F32)
        ahl = sb("ahl", [P, I, 2], F16)
        aT = sb("aT", [P, KI, P, 2], F16)
        y = sb("y", [P, H], F32)
        xg_w = xg[:, :].bitcast(F32)
        ahl_w = ahl[:, :, :].rearrange("p i a -> p (i a)").bitcast(F32)
        psG = psum("psG", [P, HALF], F32)
        psU = psum("psU", [P, HALF], F32)
        psX = psum("psX", [P, KH * P], F32)
        psA = psum("psA", [P, KI * P], F32)
        psY = psum("psY", [P, 2 * HALF], F32)

        s_past = sem("waits_passed")
        s_stage = [sem(f"chunk_in{r}") for r in range(RING)]
        s_bias = sem("bias_in")
        s_idxg = sem("gather_idx_in")
        s_idxs = sem("scatter_idx_in")
        s_xg = sem("rows_gathered")
        s_scat = sem("rows_added")
        s_added = sem("tile_added")
        s_whi = sem("weights_hi")
        s_wlo = sem("weights_lo")
        s_G = sem("gate_done")
        s_U = sem("up_done")
        s_X = sem("x_transposed")
        s_A = sem("act_transposed")
        s_Y = sem("down_done")
        s_gread = sem("gate_read")
        s_gmin = sem("gate_clipped")
        s_sig = sem("sigmoid_done")
        s_glu = sem("glu_done")
        s_uread = sem("up_read")
        s_uclip = sem("up_clipped")
        s_act = sem("act_ready")
        s_ahi = sem("act_hi")
        s_alo = sem("act_lo")
        s_xTev = sem("xT_evacuated")
        s_aTev = sem("aT_evacuated")
        s_y0 = sem("y_weighted")
        s_y = sem("y_ready")
        block = ctx.enter_context(nc.Block())

        def start_of(eng, e):
            return eng.value_load(tile_start[0:1, at(nc, e, E)], min_val=0, max_val=MAXT - 4)

        def chunk_src(q_expert, c):
            w = w_dram[c // PER_W]
            n = CHUNK // w.shape[3]
            k0 = c % PER_W * n
            return w[at(nc, q_expert, E - 1), :, k0:k0 + n, :].rearrange("o p k n -> (o p) k n")

        def load_chunk(sp, e, c):
            view = stage[:, c % RING, :].rearrange("p (k n) -> p k n", n=w_dram[c % NCHUNK // PER_W].shape[3])
            sp.dma_start(view, chunk_src(e + c // NCHUNK, c % NCHUNK)).then_inc(s_stage[c % RING], 16)

        def load_bias(sp, e, par):
            for lo, hi, src in ((0, I, g["b_gate"]), (I, 2 * I, g["b_up"]), (2 * I, 2 * I + H, g["b_down"])):
                sp.dma_start(bias[:, par, lo:hi], src[at(nc, e, E - 1), :].to_broadcast([P, hi - lo])).then_inc(s_bias, 16)

        def load_slots(sp, dst, i, done):
            row = sp.value_load(slot_row[0:1, at(nc, i, MAXT - 1)], min_val=0, max_val=slots.shape[0] - P)
            sp.dma_start(dst[:], slots[bass.ds(row, P), :]).then_inc(done, 16)

        @block.sync
        def _(sp):
            load_slots(sp, idxg, 0, s_idxg)
            for c in range(RING):
                load_chunk(sp, 0, c)
            load_bias(sp, 0, 0)
            sp.wait_ge(s_xg, 16)
            load_slots(sp, idxg, 1, s_idxg)
            for c in range(RING, NCHUNK + RING):
                sp.wait_ge(s_wlo, c - RING + 1)
                load_chunk(sp, 0, c)

            def step(i, e, t0, j, more, prev_guard):
                def prev():
                    alone(sp, s_added, i, s_past)
                    load_slots(sp, idxs, i - 1, s_idxs)
                if prev_guard is None:
                    prev()
                else:
                    with sp.If(prev_guard):
                        prev()
                sp.wait_ge(s_xg, 16 * i + 32)
                load_slots(sp, idxg, i + 2, s_idxg)
                if j is not None:
                    def loads():
                        for c in LOAD[j]:
                            alone(sp, s_wlo, NCHUNK * e + NCHUNK + c - RING + 1, s_past)
                            load_chunk(sp, e + 1, c)
                    if more[j] is None:
                        loads()
                    else:
                        with sp.If(more[j]):
                            loads()

            with sp.Fori(0, PAIRS) as pair:
                for par in range(2):
                    e = pair * 2 + par
                    t0, t1 = start_of(sp, e), start_of(sp, e + 1)
                    some = pair < PAIRS - 1
                    more = [None if par == 0 else some] * 2 + [some]
                    for j in range(MIN_TILES):
                        step(t0 + j, e, t0, j, more, pair > 0 if par == 0 and j == 0 else None)
                    if par == 0:
                        sp.wait_ge(s_y, t0 + 1)
                        load_bias(sp, e + 1, 1 - par)
                    else:
                        with sp.If(some):
                            sp.wait_ge(s_y, t0 + 1)
                            load_bias(sp, e + 1, 1 - par)
                    with sp.If(t1 > t0 + MIN_TILES):
                        with sp.Fori(t0 + MIN_TILES, t1) as i:
                            step(i, e, t0, None, None, None)
            tt = start_of(sp, E)
            alone(sp, s_added, tt, s_past)
            load_slots(sp, idxs, tt - 1, s_idxs)
            alone(sp, s_idxg, 16 * tt + 32, s_past)

        @block.gpsimd
        def _(pool):
            def gather(i):
                alone(pool, s_idxg, 16 * i + 16, s_past)
                pool.indirect_dma_start(out=xg[:], out_offset=None, in_=xn_tab[:, :],
                                        in_offset=bass.IndirectOffsetOnAxis(idxg[:, 0:1].bitcast(U32), 0)).then_inc(s_xg, 16)

            def scatter(i):
                alone(pool, s_y, i + 1, s_past)
                pool.indirect_dma_start(out=acc[:, :], out_offset=bass.IndirectOffsetOnAxis(idxs[:, 0:1].bitcast(U32), 0),
                                        in_=y[:], in_offset=None, compute_op=ALU.add).then_inc(s_scat, 16)

            pool.sem_inc(s_added, 1)
            tt = start_of(pool, E)
            gather(0)
            pool.wait_ge(s_X, 1)
            gather(1)
            pool.wait_ge(s_X, 2)
            gather(2)
            scatter(0)
            with pool.Fori(2, tt + 1) as i:
                pool.wait_ge(s_X, i + 1)
                gather(i + 1)
                pool.wait_ge(s_scat, 16 * i - 16)
                pool.sem_inc(s_added, 1)
                scatter(i - 1)
            alone(pool, s_xg, 16 * tt + 32, s_past)
            alone(pool, s_scat, 16 * tt, s_past)

        @block.scalar
        def _(act):
            def cut(e, par, c, free=None):
                act.wait_ge(s_stage[c % RING], 32 * e + 16 * (c // RING) + 16)
                if free is not None:
                    free()
                act.activation(W[:, par, HI, c * CHUNK:(c + 1) * CHUNK], stage[:, c % RING, :], ACT.Copy, scale=S_W).then_inc(s_whi, 1)

            def evac_x(i):
                act.wait_ge(s_X, i + 1)
                act.activation(xT[:].rearrange("p k q a -> p (k q a)").bitcast(F32), psX[:], ACT.Copy).then_inc(s_xTev, 1)

            def evac_a(i):
                act.wait_ge(s_A, i + 1)
                act.activation(aT[:].rearrange("p k q a -> p (k q a)").bitcast(F32), psA[:], ACT.Copy).then_inc(s_aTev, 1)

            def weigh_y(i):
                act.wait_ge(s_idxs, 16 * i + 16)
                act.wait_ge(s_added, i + 1)
                act.wait_ge(s_Y, i + 1)
                act.activation(y[:], psY[:], ACT.Copy, scale=idxs[:, 2:3].bitcast(F32)).then_inc(s_y0, 1)

            act.sem_inc(s_y0, 1)
            for c in range(NCHUNK):
                cut(0, 0, c)
            evac_x(0)

            def step(i, e, par, t0, j, more, prev_guard):
                def guarded(guard, body):
                    if guard is None:
                        body()
                    else:
                        with act.If(guard):
                            body()

                def free_gate_up():
                    alone(act, s_U, t0, s_past)

                def cut_one(n):
                    c = CUT[j][n]
                    if c == 0:
                        guarded(prev_guard, free_gate_up)
                    if c == 2 * PER_W:
                        act.wait_ge(s_Y, t0 + 1)
                    cut(e + 1, 1 - par, c)

                if j is not None:
                    guarded(more, lambda: cut_one(0))
                act.wait_ge(s_gmin, i + 1)
                act.activation(sg[:], gt[:], ACT.Sigmoid, scale=ALPHA).then_inc(s_sig, 1)
                guarded(prev_guard, lambda: evac_a(i - 1))
                if j is not None:
                    guarded(more, lambda: cut_one(1))
                evac_x(i + 1)
                act.wait_ge(s_act, i + 1)
                act.activation(ahl[:, :, HI], av[:], ACT.Copy, scale=S_ACT).then_inc(s_ahi, 1)
                guarded(prev_guard, lambda: weigh_y(i - 1))

            with act.Fori(0, PAIRS) as pair:
                for par in range(2):
                    e = pair * 2 + par
                    t0, t1 = start_of(act, e), start_of(act, e + 1)
                    for j in range(MIN_TILES):
                        step(t0 + j, e, par, t0, j, pair < PAIRS - 1 if par else None,
                             pair > 0 if par == 0 and j == 0 else None)
                    with act.If(t1 > t0 + MIN_TILES):
                        with act.Fori(t0 + MIN_TILES, t1) as i:
                            step(i, e, par, t0, None, None, None)
            tt = start_of(act, E)
            evac_a(tt - 1)
            weigh_y(tt - 1)

        @block.vector
        def _(dve):
            def cut(e, par, c):
                dve.wait_ge(s_whi, NCHUNK * e + c + 1)
                dve.scalar_tensor_tensor(out=W[:, par, LO, c * CHUNK:(c + 1) * CHUNK], in0=stage[:, c % RING, :], scalar=S_W,
                                         in1=W[:, par, HI, c * CHUNK:(c + 1) * CHUNK], op0=ALU.mult, op1=ALU.subtract).then_inc(s_wlo, 1)

            def finish_y(i, par):
                dve.wait_ge(s_y0, i + 2)
                dve.scalar_tensor_tensor(out=y[:], in0=bias[:, par, 2 * I:], scalar=idxs[:, 1:2].bitcast(F32), in1=y[:],
                                         op0=ALU.mult, op1=ALU.add).then_inc(s_y, 1)

            for c in range(NCHUNK):
                cut(0, 0, c)

            def step(i, e, par, j, more, prev_guard):
                def guarded(guard, body):
                    if guard is None:
                        body()
                    else:
                        with dve.If(guard):
                            body()

                if j == 0:
                    dve.wait_ge(s_bias, 48 * e + 48)
                dve.wait_ge(s_G, i + 1)
                dve.scalar_tensor_tensor(out=gt[:], in0=psG[:], scalar=1.0 / (S_ROWS * S_W), in1=bias[:, par, 0:I],
                                         op0=ALU.mult, op1=ALU.add).then_inc(s_gread, 1)
                dve.wait_ge(s_gread, i + 1)
                dve.tensor_scalar(gt[:], gt[:], LIMIT, None, ALU.min).then_inc(s_gmin, 1)
                if j is not None:
                    guarded(more, lambda: cut(e + 1, 1 - par, CUT[j][0]))
                dve.wait_ge(s_sig, i + 1)
                dve.tensor_tensor(gt[:], gt[:], sg[:], ALU.mult).then_inc(s_glu, 1)
                dve.wait_ge(s_U, i + 1)
                dve.scalar_tensor_tensor(out=up[:], in0=psU[:], scalar=1.0 / (S_ROWS * S_W), in1=bias[:, par, I:2 * I],
                                         op0=ALU.mult, op1=ALU.add).then_inc(s_uread, 1)
                dve.wait_ge(s_uread, i + 1)
                dve.tensor_scalar(up[:], up[:], LIMIT, -LIMIT, ALU.min, ALU.max).then_inc(s_uclip, 1)
                dve.wait_ge(s_glu, i + 1)
                dve.wait_ge(s_uclip, i + 1)
                dve.scalar_tensor_tensor(out=av[:], in0=up[:], scalar=1.0, in1=gt[:], op0=ALU.add, op1=ALU.mult).then_inc(s_act, 1)
                if j is not None:
                    guarded(more, lambda: cut(e + 1, 1 - par, CUT[j][1]))
                dve.wait_ge(s_ahi, i + 1)
                dve.scalar_tensor_tensor(out=ahl[:, :, LO], in0=av[:], scalar=S_ACT, in1=ahl[:, :, HI],
                                         op0=ALU.mult, op1=ALU.subtract).then_inc(s_alo, 1)
                guarded(prev_guard, lambda: finish_y(i - 1, 1 - par if j == 0 else par))

            with dve.Fori(0, PAIRS) as pair:
                for par in range(2):
                    e = pair * 2 + par
                    t0, t1 = start_of(dve, e), start_of(dve, e + 1)
                    for j in range(MIN_TILES):
                        step(t0 + j, e, par, j, pair < PAIRS - 1 if par else None, pair > 0 if par == 0 and j == 0 else None)
                    with dve.If(t1 > t0 + MIN_TILES):
                        with dve.Fori(t0 + MIN_TILES, t1) as i:
                            step(i, e, par, None, None, None)
            tt = start_of(dve, E)
            finish_y(tt - 1, 1)

        @block.tensor
        def _(pe):
            def weights(par, part, first, n):
                return W[:, par, part, first:first + n]

            def rows_times(ps, par, offset, done):
                for k in range(KH):
                    for n, (a, c) in enumerate(PASSES):
                        op = pe.matmul(ps[:], xT[:, k, :, a], weights(par, c, offset + k * I, I),
                                       start=k == 0 and n == 0, stop=k == KH - 1 and n == 2)
                op.then_inc(done, 1)

            def transpose_rows():
                for n in range(KH):
                    op = pe.transpose(psX[:, n * P:(n + 1) * P], xg_w[:, n * P:(n + 1) * P], ident[:])
                op.then_inc(s_X, 1)

            def transpose_act(i):
                pe.wait_ge(s_ahi, i + 1)
                pe.wait_ge(s_alo, i + 1)
                for n in range(KI):
                    op = pe.transpose(psA[:, n * P:(n + 1) * P], ahl_w[:, n * P:(n + 1) * P], ident[:])
                op.then_inc(s_A, 1)

            def down(i, par):
                pe.wait_ge(s_aTev, i + 1)
                pe.wait_ge(s_y0, i + 1)
                for h in range(2):
                    for k in range(KI):
                        for n, (a, c) in enumerate(PASSES):
                            op = pe.matmul(psY[:, h * HALF:(h + 1) * HALF], aT[:, k, :, a],
                                           weights(par, c, 2 * KH * I + k * H + h * HALF, HALF),
                                           start=k == 0 and n == 0, stop=k == KI - 1 and n == 2)
                op.then_inc(s_Y, 1)

            def step(i, e, par, first, prev_guard):
                def guarded(body):
                    if prev_guard is None:
                        body()
                    else:
                        with pe.If(prev_guard):
                            body()

                def weights_cut(chunks):
                    if first:
                        alone(pe, s_wlo, NCHUNK * e + chunks, s_past)

                pe.wait_ge(s_xTev, i + 1)
                weights_cut(PER_W)
                guarded(lambda: pe.wait_ge(s_gread, i))
                rows_times(psG, par, 0, s_G)

                def between():
                    transpose_act(i - 1)
                    pe.wait_ge(s_uread, i)
                guarded(between)
                weights_cut(2 * PER_W)
                rows_times(psU, par, KH * I, s_U)
                pe.wait_ge(s_xg, 16 * i + 32)
                transpose_rows()
                guarded(lambda: down(i - 1, 1 - par if first else par))
                weights_cut(3 * PER_W)

            pe.wait_ge(s_xg, 16)
            transpose_rows()
            with pe.Fori(0, PAIRS) as pair:
                for par in range(2):
                    e = pair * 2 + par
                    t0, t1 = start_of(pe, e), start_of(pe, e + 1)
                    step(t0, e, par, True, pair > 0 if par == 0 else None)
                    with pe.Fori(t0 + 1, t1) as i:
                        step(i, e, par, False, None)
            tt = start_of(pe, E)
            transpose_act(tt - 1)
            down(tt - 1, 1)


_INS = ["x", "ctx_1024", "L0_xattn_Wq", "L0_xattn_bq", "L0_xattn_Wk", "L0_xattn_bk", "L0_ffn_gate_w", "L0_ffn_gate_b",
        "L0_ffn_w_gate", "L0_ffn_b_gate", "L0_ffn_w_up", "L0_ffn_b_up", "L0_ffn_w_down", "L0_ffn_b_down"]


def kernel(**inputs):
    import numpy as _np
    import concourse.bacc as _bacc
    from concourse import mybir as _mybir
    from concourse.bass_utils import run_bass_kernel_spmd as _run

    nc = _bacc.Bacc("TRN2", target_bir_lowering=False, num_devices=1)
    arrays, args = {}, []
    for name in _INS:
        a = _np.ascontiguousarray(inputs[name])
        arrays[f"in_{name}"] = a
        args.append(nc.dram_tensor(f"in_{name}", a.shape, _mybir.dt.from_np(a.dtype), kind="ExternalInput").ap())
    b, l, h = inputs["x"].shape
    args.append(nc.dram_tensor("acc", (b * l + P, h), _mybir.dt.float32, kind="ExternalOutput").ap())
    xattn_moe_kernel(nc, *args)
    r = _run(nc, [arrays], core_ids=[0])
    return r.results[0]["acc"][0:b * l].reshape(b, l, h)
```

```python
from contextlib import ExitStack

import concourse.bass as bass
from concourse import mybir

ALU = mybir.AluOpType
ACT = mybir.ActivationFunctionType
AX_X = mybir.AxisListType.X
F32 = mybir.dt.float32
F16 = mybir.dt.float16
I32 = mybir.dt.int32
U32 = mybir.dt.uint32

P = 128
EPS = 1e-5
ALPHA = 1.702
LIMIT = 7.0
TOPK = 4
LO, HI = 0, 1
PASSES = ((HI, HI), (HI, LO), (LO, HI))
S_ROWS = 256.0
S_PROB = 16384.0
S_W = 256.0
S_ACT = 256.0
CHUNK = 2048
RING = 3
MIN_TILES = 3


class Tally:

    def __init__(self, sem, base=0):
        self.sem, self.base, self.n = sem, base, 0

    def inc(self, instruction, by=1):
        instruction.then_inc(self.sem, by)
        self.n += by

    def now(self):
        return self.base + self.n


def alone(eng, sem, value, passed):
    eng.wait_ge(sem, value)
    eng.sem_inc(passed, 1)


def guarded(eng, cond, body):
    if cond is None:
        body()
    else:
        with eng.If(cond):
            body()


def at(nc, value, most):
    if isinstance(value, int):
        return bass.ds(value, 1)
    return bass.ds(nc.s_assert_within(value, 0, most, skip_runtime_bounds_check_because="guarded by the loops"), 1)


def xattn_moe_kernel(nc, x, ctx_in, Wq, bq, Wk, bk, gate_w, gate_b, w_gate, b_gate, w_up, b_up,
                     w_down, b_down, acc):
    B, L, H = x.shape
    C = ctx_in.shape[2]
    D = Wq.shape[0]
    E, _, I = w_gate.shape
    T = B * L
    NT = L // P
    KH, KC, KI = H // P, C // P, I // P
    HALF = 512
    assert L == H == 1024 and D == P and acc.shape[0] == T + P
    SLOTS = E * T
    NCHUNK = 3 * KH * I // CHUNK
    MAXT = 256
    assert T * TOPK // P + E * MIN_TILES <= MAXT - 4

    x_rows = x.rearrange("b (t p) h -> b t p h", p=P)
    acc_rows = acc.rearrange("(n p) h -> n p h", p=P)
    xn_tab = nc.dram_tensor("xn_tab", (T + P, 2 * H), F16, kind="Internal").ap()
    xn_rows = xn_tab.rearrange("(n p) h -> n p h", p=P)
    slots = nc.dram_tensor("slots", (SLOTS + 2 * P, 4), I32, kind="Internal").ap()

    with ExitStack() as whole:
        ident = whole.enter_context(nc.sbuf_tensor("ident", [P, P], F32))
        tile_start = whole.enter_context(nc.sbuf_tensor("tile_start", [1, 64], I32))
        slot_row = whole.enter_context(nc.sbuf_tensor("slot_row", [1, MAXT], I32))
        W = whole.enter_context(nc.sbuf_tensor("W", [P, 2, 2, NCHUNK * CHUNK], F16))
        stage = whole.enter_context(nc.sbuf_tensor("stage", [P, RING, CHUNK], F32))
        s_stage = [whole.enter_context(nc.semaphore(f"chunk_in{r}")) for r in range(RING)]
        s_whi = whole.enter_context(nc.semaphore("weights_hi"))
        s_wlo = whole.enter_context(nc.semaphore("weights_lo"))
        w_dram = [w.rearrange("e (k p) n -> e p k n", p=P) for w in (w_gate, w_up, w_down)]

        def load_chunk(sp, e, c):
            e, r = e + c // NCHUNK, c % RING
            w = w_dram[c % NCHUNK // (NCHUNK // 3)]
            n = CHUNK // w.shape[3]
            k0 = c % (NCHUNK // 3) * n
            sp.dma_start(stage[:, r, :].rearrange("p (k n) -> p k n", k=n),
                         w[at(nc, e, E - 1), :, k0:k0 + n, :].rearrange("o p k n -> (o p) k n")).then_inc(s_stage[r], 16)

        def cut_hi(act, e, par, c):
            act.wait_ge(s_stage[c % RING], 32 * e + 16 * (c // RING) + 16)
            act.activation(W[:, par, HI, c * CHUNK:(c + 1) * CHUNK], stage[:, c % RING, :], ACT.Copy, scale=S_W).then_inc(s_whi, 1)

        def cut_lo(dve, e, par, c):
            dve.wait_ge(s_whi, NCHUNK * e + c + 1)
            dve.scalar_tensor_tensor(out=W[:, par, LO, c * CHUNK:(c + 1) * CHUNK], in0=stage[:, c % RING, :], scalar=S_W,
                                     in1=W[:, par, HI, c * CHUNK:(c + 1) * CHUNK], op0=ALU.mult, op1=ALU.subtract).then_inc(s_wlo, 1)

        attention_and_routing(nc, locals())
        experts(nc, locals())


def attention_and_routing(nc, g):
    B, L, H, C, D, E, T = g["B"], g["L"], g["H"], g["C"], g["D"], g["E"], g["T"]
    NT, KH, KC, HALF, SLOTS, MAXT = g["NT"], g["KH"], g["KC"], g["HALF"], g["SLOTS"], g["MAXT"]
    x_rows, acc_rows, xn_rows, slots = g["x_rows"], g["acc_rows"], g["xn_rows"], g["slots"]
    ident, tile_start, slot_row = g["ident"], g["tile_start"], g["slot_row"]
    ctx_in, acc, xn_tab = g["ctx_in"], g["acc"], g["xn_tab"]
    W, stage, NCHUNK, s_wlo = g["W"], g["stage"], g["NCHUNK"], g["s_wlo"]

    with ExitStack() as ctx:
        def sb(name, shape, dt):
            return ctx.enter_context(nc.sbuf_tensor(name, shape, dt))

        def psum(name, shape, dt):
            return ctx.enter_context(nc.psum_tensor(name, shape, dt))

        def sem(name):
            return ctx.enter_context(nc.semaphore(name))

        xr = sb("xr", [P, 2, H], F32)
        XT = sb("XT", [P, KH, L, 2], F16)
        xnh = sb("xnh", [P, H, 2], F16)
        ah = sb("ah", [P, 2, L, 2], F16)
        xs2 = sb("xs2", [P, H], F32)
        x2h = sb("x2h", [P, 2, H, 2], F16)
        x2T = sb("x2T", [P, KH, P], F32)
        before = sb("before", [P, P], F32)
        upto = sb("upto", [E, E], F32)
        ones = sb("ones", [P, P], F32)
        WT = sb("WT", [P, 2, KC, D], F32)
        gateT = sb("gateT", [P, KH, E], F32)
        bqk = sb("bqk", [P, 2], F32)
        gb = sb("gb", [P, E], F32)
        iota_i = sb("iota_i", [P, E], I32)
        iota_e = sb("iota_e", [P, E], F32)
        ebase = sb("ebase", [P, E], F32)
        tok = sb("tok", [P, 1], F32)
        tok_i = sb("tok_i", [P, 1], I32)
        st = sb("st", [P, 2, 6], F32)
        mv = sb("mv", [P, 2], F32)
        ve = sb("ve", [P, 2], F32)
        neg_half = sb("neg_half", [P, 1], F32)
        rstd = sb("rstd", [P, 2], F32)
        mx = sb("mx", [P, 2], F32)
        nmx = sb("nmx", [P, 2], F32)
        psm = sb("psm", [P, 2], F32)
        sc = sb("sc", [P, 2], F32)
        lg = sb("lg", [P, E], F32)
        v8 = sb("v8", [P, 2, 8], F32)
        i8 = sb("i8", [P, 8], U32)
        i4 = sb("i4", [P, TOPK], F32)
        nv0 = sb("nv0", [P, 2], F32)
        oh = sb("oh", [P, 2, TOPK, E], F32)
        mask = sb("mask", [P, 2, E], F32)
        seen = sb("seen", [P, E], F32)
        rk = sb("rk", [P, E], F32)
        junk = sb("junk", [P, TOPK, E], F32)
        dest_f = sb("dest_f", [P, TOPK], F32)
        dest = sb("dest", [P, 2, TOPK], U32)
        ex = sb("ex", [P, 2, TOPK], F32)
        es = sb("es", [P, 2], F32)
        er = sb("er", [P, 1], F32)
        wt = sb("wt", [P, TOPK], F32)
        pack = sb("pack", [P, 2, TOPK, 4], I32)
        ncol = sb("ncol", [E, 4], F32)
        ge = sb("ge", [E, MAXT], F32)
        iota_t = sb("iota_t", [E, MAXT], F32)
        iota_ti = sb("iota_ti", [E, MAXT], I32)
        rowf = sb("rowf", [1, MAXT], F32)
        assert B % 2 == 0 and L * KC == NT * C == NCHUNK * CHUNK - KH * L and CHUNK == 2 * H == 2 * L
        W_flat = W[:, :, :, :].rearrange("p a b c -> p a (b c)")
        AT = W_flat[:, :, 0:2 * KH * L].rearrange("p a (c k l) -> p a c k l", c=2, k=KH)
        cxT = W_flat[:, 0, 2 * KH * L:].bitcast(F32).rearrange("p (c l) -> p c l", c=KC)
        cx = W_flat[:, 1, 2 * KH * L:].bitcast(F32).rearrange("p (t c) -> p t c", t=NT)
        x1 = stage[:, 0, :].rearrange("p (t h) -> p t h", t=2)
        qk = stage[:, 1, :].rearrange("p (w l) -> p w l", w=2)
        prob = stage[:, 2, 0:L]
        xs = stage[:, 2, L:]
        padding = ah[:, :, :, :].rearrange("p a b c -> p (a b c)").bitcast(I32).rearrange("p (r c) -> p r c", c=4)
        wqk_in = xs[:, :].rearrange("p (w c) -> p w c", w=2)
        gate_in = prob[0:E, :]
        xnh_w = xnh[:, :, :].rearrange("p h a -> p (h a)").bitcast(F32)
        ah_w = [ah[:, j, :, :].rearrange("p h a -> p (h a)").bitcast(F32) for j in range(2)]
        XT_w = XT[:, :, :, :].rearrange("p k l a -> p (k l a)").bitcast(F32).rearrange("p (k l) -> p k l", k=KH)

        psE = psum("psE", [P, 2 * HALF], F32)
        psM = psum("psM", [P, 2 * HALF], F32)
        psT = psum("psT", [P, 2 * HALF], F32)
        psQ = psum("psQ", [P, HALF], F32)
        psR = psum("psR", [P, HALF], F32)
        psT_pairs = psT[:, :].bitcast(F16).rearrange("p (k q a) -> p a k q", k=KH, a=2)
        quarter = [psM[:, 0:HALF], psM[:, HALF:], psE[:, 0:HALF], psE[:, HALF:]]

        s_x1 = [sem(f"x1_in{t}") for t in range(2)]
        s_xr = [sem(f"xr_in{t}") for t in range(2)]
        s_ctx = sem("ctx_in")
        s_past = sem("waits_passed")
        s_small = sem("small_in")
        s_const = sem("consts")
        s_padfill = sem("pad_filled")
        s_padout = sem("pad_stored")
        s_ready = sem("dve_consts")
        s_wT = sem("w_transposed")
        s_wTev = sem("w_evacuated")
        s_x2out = [sem(f"x2_out{t}") for t in range(2)]
        s_xnout = [sem(f"xn_out{t}") for t in range(2)]
        s_slotout = [sem(f"slot_out{t}") for t in range(2)]
        s_cT = sem("ctx_transposed")
        s_cTev = sem("ctxT_evacuated")
        s_qk = sem("qk_done")
        s_qkev = sem("qk_evacuated")
        s_E = sem("energy_done")
        s_nmx = sem("negmax_ready")
        s_exp = sem("exp_done")
        s_sc = sem("prob_scale_ready")
        s_ahi = sem("prob_hi")
        s_alo = sem("prob_lo")
        s_AT = sem("prob_transposed")
        s_ATev = sem("probT_evacuated")
        s_var = [sem(f"variance{n}_ready") for n in (1, 2)]
        s_rstd = [sem(f"rstd{n}_ready") for n in (1, 2)]
        s_xs = sem("ln1_ready")
        s_xhi = sem("ln1_hi")
        s_xlo = sem("ln1_lo")
        s_xT = sem("ln1_transposed")
        s_xTev = sem("ln1T_evacuated")
        s_xm = sem("xm_done")
        s_x2 = sem("x2_ready")
        s_xs2 = sem("ln2_ready")
        s_hi2 = sem("ln2_hi")
        s_lo2 = sem("ln2_lo")
        s_x2T = sem("ln2_transposed")
        s_x2Tev = sem("ln2T_evacuated")
        s_lgt = sem("logits_done")
        s_lgev = sem("logits_read")
        s_nv0 = sem("top1_ready")
        s_ex = sem("weights_exp")
        s_mask = sem("mask_ready")
        s_rank = sem("rank_done")
        s_seen = sem("seen_ready")
        s_pack = sem("pack_ready")
        s_ln = [sem(f"ln{n}_chain") for n in (1, 2)]
        s_soft = sem("softmax_chain")
        s_top = sem("topk_chain")
        s_slot = sem("slot_chain")
        s_once = sem("dve_once")
        s_tail = sem("tail_pe")
        s_tailv = sem("tail_dve")
        block = ctx.enter_context(nc.Block())

        CTX_STEPS = range(2, 2 + NT // 2)

        def batch(bk):
            return bk[0] + bk[1]

        def following(bk):
            return bk[0], bk[1] + 1

        def per(n, bk, offset):
            return bk[0] * n + (bk[1] * n + offset)

        def tile(bk, offset):
            return per(NT, bk, offset)

        def first(bk):
            return isinstance(bk[0], int) and batch(bk) == 0

        def lagged(bk, s, lag):
            if bk is None:
                return None
            if s >= lag:
                return (bk, s - lag) if s - lag < NT else None
            return None if first(bk) else ((bk[0], bk[1] - 1), NT + s - lag)

        def par(bk):
            b = batch(bk)
            return slice(b % 2, b % 2 + 1) if isinstance(b, int) else at(nc, b % 2, 1)

        def schedule(eng, step, prepare):
            prepare()
            for s in range(NT):
                step(s, (0, 0), None, None)
            for s in range(2):
                step(s, (0, 1), (0, 0), None)
            with eng.Fori(0, B - 1) as b:
                more = b < B - 2
                for s in range(2, NT):
                    step(s, (b, 1), (b, 0), more)
                for s in range(2):
                    step(s, (b, 2), (b, 1), more)
            for s in range(2, NT + 2):
                step(s, None, (B - 1, 0), None)

        def product_of(s, b1):
            return psE if b1 is None and s % 2 else psM

        @block.sync
        def _(sp):
            for t in range(2):
                sp.sem_inc(s_xnout[t], 16)

            def load_x(dst, sems, b, t):
                sp.dma_start(dst[:, t % 2, :], x_rows[at(nc, b, B - 1), t].rearrange("o p h -> (o p) h")).then_inc(sems[t % 2], 16)

            def load_ctx(b):
                sp.dma_start(cx[:], ctx_in[at(nc, b, B - 1)].rearrange("o (t p) c -> p (o t) c", p=P)).then_inc(s_ctx, 16)

            sp.dma_start(wqk_in[:, 0, :], g["Wq"]).then_inc(s_small, 16)
            sp.dma_start(wqk_in[:, 1, :], g["Wk"]).then_inc(s_small, 16)
            sp.dma_start(gate_in, g["gate_w"]).then_inc(s_small, 16)
            sp.dma_start(bqk[:, 0:1], g["bq"].rearrange("(d o) -> d o", o=1)).then_inc(s_small, 16)
            sp.dma_start(bqk[:, 1:2], g["bk"].rearrange("(d o) -> d o", o=1)).then_inc(s_small, 16)
            sp.dma_start(gb[:], g["gate_b"].rearrange("(o e) -> o e", o=1).to_broadcast([P, E])).then_inc(s_small, 16)
            load_ctx(0)
            for t in range(2):
                load_x(x1, s_x1, 0, t)
            sp.wait_ge(s_padfill, 2)
            half = SLOTS // P // 2
            for part in range(2):
                sp.dma_start(slots[0:SLOTS, :].rearrange("(p r) c -> p r c", p=P)[:, part * half:(part + 1) * half, :],
                             padding).then_inc(s_padout, 16)
            sp.dma_start(slots[SLOTS:SLOTS + 2 * P, :].rearrange("(o r) c -> o r c", o=1),
                         padding[0:1, 0:2 * P, :]).then_inc(s_padout, 16)
            zero = x2T[:, :, :].rearrange("p k q -> p (k q)")
            sp.dma_start(xn_rows[T // P], zero.bitcast(F16)).then_inc(s_padout, 16)
            sp.dma_start(acc_rows[T // P], zero).then_inc(s_padout, 16)
            for t in range(2):
                load_x(xr, s_xr, 0, t)

            def prepare():
                sp.wait_ge(s_cT, NT // 2)
                load_ctx(1)

            def step(s, b1, b2, more):
                if b1 is None and s == 2:
                    for done in (s_xs, s_alo, s_xlo, s_E):
                        sp.wait_ge(done, B * NT)
                    for c in range(RING):
                        g["load_chunk"](sp, 0, c)

                def next_x1():
                    alone(sp, s_xs, tile(b1, s + 1), s_past)
                    if s < NT - 2:
                        load_x(x1, s_x1, batch(b1), s + 2)
                    else:
                        load_x(x1, s_x1, batch(following(b1)), s + 2 - NT)

                def next_ctx():
                    alone(sp, s_cT, per(NT // 2, b1, NT), s_past)
                    load_ctx(batch(b1) + 2)

                if b1 is not None:
                    guarded(sp, more if s < 2 or s >= NT - 2 else None, next_x1)
                    if s == NT - 2:
                        guarded(sp, None if first(b1) else b1[0] < B - 3, next_ctx)
                if b2 is not None and s < NT:
                    n = tile(b2, s)
                    sp.wait_ge(s_x2, tile(b2, s + 1))
                    sp.dma_start(acc_rows[bass.ds(n, 1)].rearrange("o p h -> (o p) h"), xr[:, s % 2, :]).then_inc(s_x2out[s % 2], 16)
                    sp.wait_ge(s_lo2, tile(b2, s + 1))
                    sp.dma_start(xn_rows[bass.ds(n, 1)].rearrange("o p h -> (o p) h"),
                                 x2h[:, s % 2].rearrange("p h a -> p (h a)")).then_inc(s_xnout[s % 2], 16)
                    if s < NT - 2 or b1 is not None:
                        alone(sp, s_x2out[s % 2], per(8 * NT, b2, 16 * (s // 2 + 1)), s_past)
                        load_x(xr, s_xr, batch(b2 if s < NT - 2 else following(b2)), (s + 2) % NT)
                    if b1 is None:
                        sp.wait_ge(s_wlo, s - 1)
                        g["load_chunk"](sp, 0, s - 2 + RING)

            schedule(sp, step, prepare)
            for t in range(2):
                sp.wait_ge(s_x2out[t], 16 * B * NT // 2)
            for t in range(2):
                sp.wait_ge(s_xnout[t], 16 * (B * NT // 2 + 1))

        @block.gpsimd
        def _(pool):
            pool.memset(ident[:], 0.0).then_inc(s_const, 1)
            pool.memset(ones[:], 1.0).then_inc(s_const, 1)
            pool.memset(before[:], 1.0).then_inc(s_const, 1)
            pool.memset(upto[:], 1.0).then_inc(s_const, 1)
            pool.memset(seen[:], 0.0).then_inc(s_const, 1)
            pool.wait_ge(s_const, 5)
            pool.affine_select(out=ident[:], in_=ident[:], compare_op=ALU.not_equal, fill=1.0, base=0,
                               pattern=[[-1, P]], channel_multiplier=1).then_inc(s_const, 1)
            pool.affine_select(out=before[:], in_=before[:], compare_op=ALU.is_gt, fill=0.0, base=0,
                               pattern=[[1, P]], channel_multiplier=-1).then_inc(s_const, 1)
            pool.affine_select(out=upto[:], in_=upto[:], compare_op=ALU.is_ge, fill=0.0, base=0,
                               pattern=[[1, E]], channel_multiplier=-1).then_inc(s_const, 1)
            pool.iota(iota_i[:], pattern=[[1, E]], base=0, channel_multiplier=0).then_inc(s_const, 1)
            pool.iota(iota_ti[:], pattern=[[1, MAXT]], base=0, channel_multiplier=0).then_inc(s_const, 1)
            pool.iota(tok_i[:], pattern=[[0, 1]], base=0, channel_multiplier=1).then_inc(s_const, 1)
            pool.memset(padding, 0).then_inc(s_const, 1)
            pool.memset(x2T[:], 0.0).then_inc(s_padfill, 1)
            pool.memset(neg_half[:], -0.5).then_inc(s_const, 1)
            pool.memset(pack[:], 0).then_inc(s_const, 1)
            pool.wait_ge(s_const, 14)
            pool.iota(padding[:, :, 0].rearrange("p (a l) -> p a l", l=P), pattern=[[0, padding.shape[1] // P], [1, P]],
                      base=T, channel_multiplier=0).then_inc(s_padfill, 1)
            def inverse_root(which, nth):
                pool.wait_ge(s_var[which], nth)
                pool.tensor_tensor(out=rstd[:, which:which + 1], in0=ve[:, which:which + 1], in1=neg_half[:],
                                   op=ALU.pow).then_inc(s_rstd[which], 1)

            def step(s, b1, b2, more):
                if b2 is not None and first(b2) and s == 1:
                    pool.wait_ge(s_padout, 16 * 5)
                if b1 is not None:
                    guarded(pool, more if s < 2 else None, lambda: inverse_root(0, tile(b1, s + 1)))
                done = lagged(b2, s, 2)
                if done:
                    bt, n = done
                    alone(pool, s_pack, tile(bt, n + 1), s_past)
                    for k in range(TOPK):
                        pool.indirect_dma_start(
                            out=slots[:, :], out_offset=bass.IndirectOffsetOnAxis(dest[:, n % 2, k:k + 1], 0),
                            in_=pack[:, n % 2, k, :], in_offset=None).then_inc(s_slotout[n % 2], 16)
                if b2 is not None and s < NT:
                    inverse_root(1, tile(b2, s + 1))

            schedule(pool, step, lambda: None)
            for t in range(2):
                pool.wait_ge(s_slotout[t], 16 * TOPK * (B * NT // 2))

        @block.scalar
        def _(act):
            for n in range(2 * KC + KH):
                act.wait_ge(s_wT, n + 1)
                if n < 2 * KC:
                    act.activation(WT[:, n // KC, n % KC, :], psT[:, n % 2 * HALF:n % 2 * HALF + D], ACT.Copy).then_inc(s_wTev, 1)
                else:
                    act.activation(gateT[:, n - 2 * KC, :], psT[:, n % 2 * HALF:n % 2 * HALF + E], ACT.Copy).then_inc(s_wTev, 1)

            def context(bk, pair):
                act.wait_ge(s_cT, per(NT // 2, bk, pair + 1))
                act.activation(cxT[:, :, pair * 2 * P:(pair + 1) * 2 * P].rearrange("p c (t q) -> p t c q", t=2),
                               psT[:, :].rearrange("p (t c q) -> p t c q", t=2, c=KC), ACT.Copy).then_inc(s_cTev, 1)

            def prepare():
                for pair in range(NT // 2):
                    context((0, 0), pair)
                act.wait_ge(s_padout, 16 * 5)

            def step(s, b1, b2, more):
                own = more if s < 2 else None
                late = lagged(b2, s, 1)

                def exponent():
                    act.wait_ge(s_nmx, tile(b1, s + 1))
                    act.activation(prob[:], psE[:], ACT.Exp, bias=nmx[:, 0:1], accum_out=psm[:, 0:1]).then_inc(s_exp, 1)

                def attention_out(bk, m):
                    act.wait_ge(s_AT, tile(bk, m + 1))
                    dst = AT[:, par(bk), :, :, m * P:(m + 1) * P].rearrange("p o a k q -> p (o a) k q")
                    act.activation(dst, psT_pairs, ACT.Copy).then_inc(s_ATev, 1)

                def hi_parts():
                    act.wait_ge(s_sc, tile(b1, s + 1))
                    act.activation(ah[:, s % 2, :, HI], prob[:], ACT.Copy, scale=sc[:, 0:1]).then_inc(s_ahi, 1)
                    act.wait_ge(s_xs, tile(b1, s + 1))
                    act.activation(xnh[:, :, HI], xs[:], ACT.Copy, scale=S_ROWS).then_inc(s_xhi, 1)

                def rows_out(s):
                    act.wait_ge(s_xT, tile(b1, s + 1))
                    act.activation(XT_w[:, :, s * P:(s + 1) * P], psT[:, :].rearrange("p (k q) -> p k q", q=P),
                                   ACT.Copy).then_inc(s_xTev, 1)

                if b1 is not None:
                    guarded(act, own, exponent)
                    if s >= 1 and b2 is not None:
                        guarded(act, own, lambda: attention_out(b1, s - 1))
                    elif s >= 1:
                        if s - 1 in CTX_STEPS:
                            context(following(b1), s - 1 - CTX_STEPS[0])
                        rows_out(s - 1)
                if b2 is not None and s == 0:
                    attention_out(b2, NT - 1)
                if late:
                    bt, n = late
                    act.wait_ge(s_xnout[n % 2], per(8 * NT, bt, 16 * (n // 2 + 1)))
                    act.wait_ge(s_xs2, tile(bt, n + 1))
                    act.activation(x2h[:, n % 2, :, HI], xs2[:], ACT.Copy, scale=S_ROWS).then_inc(s_hi2, 1)
                if b1 is not None:
                    guarded(act, own, hi_parts)
                    if s >= 1 and b2 is None:
                        attention_out(b1, s - 1)
                if late:
                    act.wait_ge(s_x2T, tile(bt, n + 1))
                    act.activation(x2T[:], psT[:, :].rearrange("p (k q) -> p k q", q=P), ACT.Copy).then_inc(s_x2Tev, 1)
                if b1 is not None and b2 is not None:
                    if s in CTX_STEPS:
                        guarded(act, more, lambda: context(following(b1), s - CTX_STEPS[0]))
                    guarded(act, own, lambda: rows_out(s))
                elif b1 is not None and s == NT - 1:
                    rows_out(s)
                if late:
                    act.wait_ge(s_nv0, tile(bt, n + 1))
                    act.activation(ex[:, n % 2, :], v8[:, n % 2, 0:TOPK], ACT.Exp, bias=nv0[:, n % 2:n % 2 + 1],
                                   accum_out=es[:, n % 2:n % 2 + 1]).then_inc(s_ex, 1)
                if b1 is None and 3 <= s < NT:
                    if s == 3:
                        act.wait_ge(s_xm, (B - 1) * NT)
                        act.wait_ge(s_qk, 4 * B)
                    g["cut_hi"](act, 0, 0, s - 3)

            schedule(act, step, prepare)
            for c in range(NT - 3, NCHUNK):
                g["cut_hi"](act, 0, 0, c)

        @block.tensor
        def _(pe):
            pe.wait_ge(s_const, 8)
            pe.wait_ge(s_small, 16 * 6)
            for n in range(2 * KC + KH):
                if n >= 2:
                    pe.wait_ge(s_wTev, n - 1)
                dst = psT[:, n % 2 * HALF:]
                if n < 2 * KC:
                    pe.transpose(dst[:, 0:D], wqk_in[:, n // KC, n % KC * P:(n % KC + 1) * P], ident[:]).then_inc(s_wT, 1)
                else:
                    k = n - 2 * KC
                    pe.transpose(dst[:, 0:E], gate_in[:, k * P:(k + 1) * P], ident[0:E, 0:E]).then_inc(s_wT, 1)
            pe.wait_ge(s_wTev, 2 * KC + KH)
            pe.wait_ge(s_ready, 1)

            def energies(m):
                for h in range(2):
                    op = pe.matmul(psE[:, h * HALF:(h + 1) * HALF], qk[:, 0, m * P:(m + 1) * P],
                                   qk[:, 1, h * HALF:(h + 1) * HALF], start=True, stop=True)
                op.then_inc(s_E, 1)

            def transpose_words(src, done):
                for k in range(KH):
                    op = pe.transpose(psT[:, k * P:(k + 1) * P], src[:, k * P:(k + 1) * P], ident[:])
                op.then_inc(done, 1)

            def context(bk, pair):
                if pair == 0:
                    alone(pe, s_ctx, per(16, bk, 16), s_past)
                for t in range(2):
                    for c in range(KC):
                        op = pe.transpose(psT[:, t * HALF + c * P:t * HALF + (c + 1) * P],
                                          cx[:, 2 * pair + t, c * P:(c + 1) * P], ident[:])
                op.then_inc(s_cT, 1)

            def queries_and_keys(bk):
                pe.wait_ge(s_cTev, per(NT // 2, bk, NT // 2))
                for n in range(4):
                    for c in range(KC):
                        op = pe.matmul(quarter[n], WT[:, n // 2, c, :], cxT[:, c, n % 2 * HALF:(n % 2 + 1) * HALF],
                                       start=c == 0, stop=c == KC - 1)
                    op.then_inc(s_qk, 1)
                pe.wait_ge(s_qkev, per(4, bk, 4))
                energies(0)

            def prepare():
                for pair in range(NT // 2):
                    if pair:
                        pe.wait_ge(s_cTev, pair)
                    context((0, 0), pair)
                queries_and_keys((0, 0))

            def product(out, bk, t, h, blocks):
                for k in blocks:
                    for n, (a, c) in enumerate(PASSES):
                        op = pe.matmul(out[:, h * HALF:(h + 1) * HALF], XT[:, k, t * P:(t + 1) * P, a],
                                       AT[:, par(bk), c, k, h * HALF:(h + 1) * HALF].rearrange("p o q -> p (o q)"),
                                       start=k == 0 and n == 0, stop=k == KH - 1 and n == 2)
                return op

            def step(s, b1, b2, more):
                own = more if s < 2 else None
                late = lagged(b2, s, 1)

                def next_energies():
                    if s < NT - 1:
                        pe.wait_ge(s_exp, tile(b1, s + 1))
                        energies(s + 1)

                if b1 is not None and b2 is None:
                    next_energies()
                if b1 is not None and s >= 1:
                    def attention_in():
                        alone(pe, s_xTev, tile(b1, s), s_past)
                        pe.wait_ge(s_alo, tile(b1, s))
                        transpose_words(ah_w[(s - 1) % 2], s_AT)
                    guarded(pe, own, attention_in)
                if b2 is not None and s == 0:
                    alone(pe, s_xTev, tile(b2, NT), s_past)
                    pe.wait_ge(s_alo, tile(b2, NT))
                    transpose_words(ah_w[(NT - 1) % 2], s_AT)
                if b2 is not None and s < NT:
                    if b1 is None and s > 2:
                        pe.wait_ge(s_exp, B * NT)
                        pe.wait_ge(s_x2, tile(b2, s - 1))
                    elif s > 0 or not first(b2):
                        pe.wait_ge(s_x2, tile(b2, s))
                    if s == 0:
                        pe.wait_ge(s_ATev, tile(b2, NT - 1))
                    product(product_of(s, b1), b2, s, 0, range(KH))
                if b2 is not None and s == 0:
                    alone(pe, s_ATev, tile(b2, NT), s_past)
                if late:
                    bt, n = late
                    if b1 is not None and s >= 1:
                        guarded(pe, own, lambda: alone(pe, s_ATev, tile(b1, s), s_past))
                    pe.wait_ge(s_xs2, tile(bt, n + 1))
                    transpose_words(xs2, s_x2T)
                if b2 is not None and s < NT:
                    product(product_of(s, b1), b2, s, 1, range(KH // 2))
                if late:
                    pe.wait_ge(s_x2Tev, tile(bt, n + 1))
                    if n >= 1 or not first(bt):
                        pe.wait_ge(s_lgev, tile(bt, n))
                    for k in range(KH):
                        op = pe.matmul(psR[:, 0:E], x2T[:, k, :], gateT[:, k, :], start=k == 0, stop=k == KH - 1)
                    op.then_inc(s_lgt, 1)
                if b1 is not None:
                    if b2 is None and s >= 1:
                        pe.wait_ge(s_ATev, tile(b1, s))
                    if s in CTX_STEPS:
                        guarded(pe, more, lambda: context(following(b1), s - CTX_STEPS[0]))
                if b2 is not None and s < NT:
                    product(product_of(s, b1), b2, s, 1, range(KH // 2, KH)).then_inc(s_xm, 1)
                if b1 is not None:
                    if s in CTX_STEPS:
                        guarded(pe, more, lambda: alone(pe, s_cTev, per(NT // 2, following(b1), s - CTX_STEPS[0] + 1), s_past))

                    def rows_in():
                        pe.wait_ge(s_xlo, tile(b1, s + 1))
                        transpose_words(xnh_w, s_xT)
                        if b2 is not None:
                            next_energies()
                    guarded(pe, own, rows_in)
                    if s == NT - 1:
                        def next_batch():
                            alone(pe, s_exp, tile(b1, NT), s_past)
                            if b2 is not None:
                                alone(pe, s_x2, tile(b2, NT), s_past)
                            queries_and_keys(following(b1))
                        guarded(pe, more, next_batch)
                if late:
                    pe.wait_ge(s_mask, tile(bt, n + 1))
                    pe.wait_ge(s_seen, tile(bt, n + 1))
                    pe.matmul(psQ[:, 0:E], before[:], mask[:, n % 2, :], start=True, stop=False)
                    pe.matmul(psQ[:, 0:E], ones[:], seen[:], start=False, stop=True).then_inc(s_rank, 1)

            schedule(pe, step, prepare)
            pe.wait_ge(s_seen, B * NT + 1)
            pe.matmul(psQ[0:E, 0:1], seen[:], ones[:, 0:1], start=True, stop=True).then_inc(s_tail, 1)
            pe.wait_ge(s_tailv, 1)
            pe.matmul(psR[0:E, 0:1], upto[:], ncol[:, 0:1], start=True, stop=True).then_inc(s_tail, 1)
            pe.wait_ge(s_tailv, 2)
            pe.matmul(psE[0:1, 0:E], ncol[:, 0:1], upto[:], start=True, stop=True).then_inc(s_tail, 1)
            pe.matmul(psM[0:1, 0:MAXT], ones[0:E, 0:1], ge[:], start=True, stop=True).then_inc(s_tail, 1)

        @block.vector
        def _(dve):
            def link(tally, ins):
                tally.inc(ins)
                dve.wait_ge(tally.sem, tally.now())

            def layernorm(which, out, src, ready, n):
                v = Tally(s_ln[which], n * 3)
                for h in range(2):
                    v.inc(dve.bn_stats(st[:, h, :], src[:, h * HALF:(h + 1) * HALF]))
                alone(dve, v.sem, v.now(), s_past)
                link(v, dve.bn_aggr(mv[:], st[:, :, :]))
                dve.tensor_scalar(ve[:, which:which + 1], mv[:, 1:2], EPS, None, ALU.add).then_inc(s_var[which], 1)
                dve.wait_ge(s_rstd[which], n + 1)
                dve.tensor_scalar(out, src, mv[:, 0:1], rstd[:, which:which + 1], ALU.subtract, ALU.mult).then_inc(ready, 1)

            first = Tally(s_once)
            dve.wait_ge(s_const, 11)
            link(first, dve.tensor_copy(iota_e[:], iota_i[:]))
            link(first, dve.tensor_scalar(ebase[:], iota_e[:], float(T), None, ALU.mult))
            link(first, dve.tensor_copy(iota_t[:], iota_ti[:]))
            link(first, dve.tensor_copy(tok[:], tok_i[:]))
            dve.memset(lg[:], 0.0).then_inc(s_ready, 1)
            dve.memset(psm[:], 0.0).then_inc(s_seen, 1)
            dve.wait_ge(s_small, 16 * 6)
            dve.wait_ge(s_wTev, 2 * KC + KH)

            def queries_and_keys(bk):
                for n in range(4):
                    dve.wait_ge(s_qk, per(4, bk, n + 1))
                    dve.tensor_scalar(qk[:, n // 2, n % 2 * HALF:(n % 2 + 1) * HALF], quarter[n],
                                      bqk[:, n // 2:n // 2 + 1], None, ALU.add).then_inc(s_qkev, 1)

            def step(s, b1, b2, more):
                own = more if s < 2 else None

                def maximum_and_norm():
                    v = Tally(s_soft, tile(b1, s) * 2)
                    dve.wait_ge(s_E, tile(b1, s + 1))
                    link(v, dve.reduce_max(mx[:, 0:1], psE[:], axis=AX_X))
                    dve.tensor_scalar(nmx[:, 0:1], mx[:, 0:1], -1.0, None, ALU.mult).then_inc(s_nmx, 1)
                    dve.wait_ge(s_x1[s % 2], per(8 * NT, b1, 16 * (s // 2 + 1)))
                    layernorm(0, xs[:], x1[:, s % 2, :], s_xs, tile(b1, s))
                    dve.wait_ge(s_exp, tile(b1, s + 1))
                    link(v, dve.reciprocal(sc[:, 1:2], psm[:, 0:1]))
                    dve.tensor_scalar(sc[:, 0:1], sc[:, 1:2], S_PROB, None, ALU.mult).then_inc(s_sc, 1)
                    assert v.n == 2

                def lo_parts():
                    dve.wait_ge(s_ahi, tile(b1, s + 1))
                    dve.wait_ge(s_sc, tile(b1, s + 1))
                    dve.scalar_tensor_tensor(out=ah[:, s % 2, :, LO], in0=prob[:], scalar=sc[:, 0:1],
                                             in1=ah[:, s % 2, :, HI], op0=ALU.mult, op1=ALU.subtract).then_inc(s_alo, 1)
                    dve.wait_ge(s_xhi, tile(b1, s + 1))
                    dve.scalar_tensor_tensor(out=xnh[:, :, LO], in0=xs[:], scalar=S_ROWS, in1=xnh[:, :, HI],
                                             op0=ALU.mult, op1=ALU.subtract).then_inc(s_xlo, 1)

                if b1 is not None:
                    guarded(dve, own, maximum_and_norm)
                late, latest = lagged(b2, s, 1), lagged(b2, s, 2)
                if late:
                    bt, n = late
                    dve.wait_ge(s_hi2, tile(bt, n + 1))
                    dve.scalar_tensor_tensor(out=x2h[:, n % 2, :, LO], in0=xs2[:], scalar=S_ROWS, in1=x2h[:, n % 2, :, HI],
                                             op0=ALU.mult, op1=ALU.subtract).then_inc(s_lo2, 1)
                if latest:
                    bt, n = latest
                    j = n % 2
                    v = Tally(s_slot, tile(bt, n) * 11)
                    dve.wait_ge(s_rank, tile(bt, n + 1))
                    link(v, dve.tensor_tensor(rk[:], psQ[:, 0:E], ebase[:], ALU.add))
                    for k in range(TOPK):
                        v.inc(dve.tensor_tensor_reduce(out=junk[:, k, :], in0=oh[:, j, k, :], in1=rk[:], scale=1.0, scalar=0.0,
                                                       op0=ALU.mult, op1=ALU.add, accum_out=dest_f[:, k:k + 1]))
                    alone(dve, v.sem, v.now(), s_past)
                    if n < 2 and not isinstance(bt[0], int):
                        with dve.If(bt[0] > 0):
                            alone(dve, s_slotout[j], per(8 * NT * TOPK, bt, 0), s_past)
                    else:
                        dve.wait_ge(s_slotout[j], per(8 * NT * TOPK, bt, 16 * TOPK * (n // 2)))
                    v.inc(dve.tensor_copy(dest[:, j, :], dest_f[:]))
                    dve.wait_ge(s_ex, tile(bt, n + 1))
                    link(v, dve.reciprocal(er[:], es[:, j:j + 1]))
                    link(v, dve.tensor_scalar(wt[:], ex[:, j, :], er[:], None, ALU.mult))
                    v.inc(dve.tensor_copy(pack[:, j, :, 1].bitcast(F32), wt[:]))
                    v.inc(dve.tensor_scalar(pack[:, j, :, 2].bitcast(F32), wt[:], 1.0 / (S_ACT * S_W), None, ALU.mult))
                    v.inc(dve.tensor_copy(pack[:, j, :, 0], tok[:].to_broadcast([P, TOPK])))
                    dve.wait_ge(v.sem, v.now())
                    dve.tensor_tensor(seen[:], seen[:], mask[:, j, :], ALU.add).then_inc(s_seen, 1)
                    dve.tensor_scalar(tok[:], tok[:], float(P), None, ALU.add).then_inc(s_pack, 1)
                    alone(dve, s_pack, tile(bt, n + 1), s_past)
                    assert v.n == 11
                if b1 is not None:
                    guarded(dve, own, lo_parts)
                if late:
                    bt, n = late
                    j = n % 2
                    v = Tally(s_top, tile(bt, n) * 7)
                    dve.wait_ge(s_lgt, tile(bt, n + 1))
                    dve.tensor_tensor(lg[:], psR[:, 0:E], gb[:], ALU.add).then_inc(s_lgev, 1)
                    alone(dve, s_lgev, tile(bt, n + 1), s_past)
                    link(v, dve.max(v8[:, j, :], lg[:]))
                    dve.tensor_scalar(nv0[:, j:j + 1], v8[:, j, 0:1], -1.0, None, ALU.mult).then_inc(s_nv0, 1)
                    link(v, dve.max_index(i8[:], v8[:, j, :], lg[:]))
                    link(v, dve.tensor_copy(i4[:], i8[:, 0:TOPK]))
                    for k in range(TOPK):
                        v.inc(dve.tensor_scalar(oh[:, j, k, :], iota_e[:], i4[:, k:k + 1], None, ALU.is_equal))
                    dve.wait_ge(v.sem, v.now())
                    dve.tensor_reduce(mask[:, j, :], oh[:, j].rearrange("p k e -> p e k"), AX_X, ALU.add).then_inc(s_mask, 1)
                    assert v.n == 7
                if b2 is not None and s < NT:
                    dve.wait_ge(s_xr[s % 2], per(8 * NT, b2, 16 * (s // 2 + 1)))
                    dve.wait_ge(s_xm, tile(b2, s + 1))
                    dve.scalar_tensor_tensor(out=xr[:, s % 2, :], in0=product_of(s, b1)[:], scalar=1.0 / (S_ROWS * S_PROB),
                                             in1=xr[:, s % 2, :], op0=ALU.mult, op1=ALU.add).then_inc(s_x2, 1)
                    alone(dve, s_x2, tile(b2, s + 1), s_past)
                    if late:
                        alone(dve, s_x2T, tile(b2, s), s_past)
                    layernorm(1, xs2[:], xr[:, s % 2, :], s_xs2, tile(b2, s))
                    if b1 is None and s >= 3:
                        g["cut_lo"](dve, 0, 0, s - 3)
                if b1 is not None and s == NT - 1:
                    guarded(dve, more, lambda: queries_and_keys(following(b1)))

            schedule(dve, step, lambda: queries_and_keys((0, 0)))
            z = Tally(s_once, first.n)
            dve.wait_ge(s_tail, 1)
            link(z, dve.tensor_copy(ncol[:, 3:4], psQ[0:E, 0:1]))
            link(z, dve.tensor_scalar(ge[:, 0:T // P], iota_t[:, 0:T // P], float(P), ncol[:, 3:4], ALU.mult, ALU.is_lt))
            link(z, dve.reduce_sum(ncol[:, 2:3], ge[:, 0:T // P], axis=AX_X))
            dve.tensor_scalar(ncol[:, 0:1], ncol[:, 2:3], float(MIN_TILES), None, ALU.max).then_inc(s_tailv, 1)
            dve.wait_ge(s_tailv, 1)
            link(z, dve.tensor_scalar(ncol[:, 1:2], ncol[:, 0:1], -float(P), float(T), ALU.mult, ALU.add))
            dve.wait_ge(s_tail, 2)
            link(z, dve.tensor_copy(ncol[:, 2:3], psR[0:E, 0:1]))
            link(z, dve.tensor_scalar(ge[:], iota_t[:], ncol[:, 2:3], ncol[:, 1:2], ALU.is_ge, ALU.mult))
            dve.memset(tile_start[:], 0).then_inc(s_tailv, 1)
            dve.wait_ge(s_tailv, 2)
            dve.wait_ge(s_tail, 3)
            dve.tensor_copy(tile_start[0:1, 1:E + 1], psE[0:1, 0:E]).then_inc(s_tailv, 1)
            dve.wait_ge(s_tail, 4)
            link(z, dve.scalar_tensor_tensor(out=rowf[:], in0=iota_t[0:1, :], scalar=float(P), in1=psM[0:1, 0:MAXT],
                                             op0=ALU.mult, op1=ALU.add))
            dve.tensor_copy(slot_row[:], rowf[:]).then_inc(s_tailv, 1)
            dve.wait_ge(s_tailv, 4)
            for c in range(NT - 3, NCHUNK):
                g["cut_lo"](dve, 0, 0, c)


def experts(nc, g):
    H, E, I, T = g["H"], g["E"], g["I"], g["T"]
    KH, KI, HALF, NCHUNK, MAXT = g["KH"], g["KI"], g["HALF"], g["NCHUNK"], g["MAXT"]
    slots, xn_tab, acc = g["slots"], g["xn_tab"], g["acc"]
    ident, tile_start, slot_row = g["ident"], g["tile_start"], g["slot_row"]
    W, stage, s_whi, s_wlo = g["W"], g["stage"], g["s_whi"], g["s_wlo"]
    load_chunk, cut_hi, cut_lo = g["load_chunk"], g["cut_hi"], g["cut_lo"]
    PAIRS = E // 2
    PER_W = NCHUNK // 3
    CUT = [[0, 1], [2, 3], [4, 5]]
    LOAD = [[3, 4], [5], [6, 7, 8]]
    assert NCHUNK == 6 and len(CUT) == MIN_TILES

    with ExitStack() as ctx:
        def sb(name, shape, dt):
            return ctx.enter_context(nc.sbuf_tensor(name, shape, dt))

        def psum(name, shape, dt):
            return ctx.enter_context(nc.psum_tensor(name, shape, dt))

        def sem(name):
            return ctx.enter_context(nc.semaphore(name))

        bias = sb("bias", [P, 2, 2 * I + H], F32)
        idxg = sb("idxg", [P, 4], I32)
        idxs = sb("idxs", [P, 4], I32)
        xg = sb("xg", [P, 2 * H], F16)
        xT = sb("xT", [P, KH, P, 2], F16)
        gt = sb("gt", [P, I], F32)
        sg = sb("sg", [P, I], F32)
        up = sb("up", [P, I], F32)
        av = sb("av", [P, I], F32)
        ahl = sb("ahl", [P, I, 2], F16)
        aT = sb("aT", [P, KI, P, 2], F16)
        y = sb("y", [P, H], F32)
        xg_w = xg[:, :].bitcast(F32)
        ahl_w = ahl[:, :, :].rearrange("p i a -> p (i a)").bitcast(F32)
        psG = psum("psG", [P, HALF], F32)
        psU = psum("psU", [P, HALF], F32)
        psX = psum("psX", [P, KH * P], F32)
        psA = psum("psA", [P, KI * P], F32)
        psY = psum("psY", [P, 2 * HALF], F32)

        s_past = sem("waits_passed")
        s_bias = sem("bias_in")
        s_idxg = sem("gather_idx_in")
        s_idxs = sem("scatter_idx_in")
        s_xg = sem("rows_gathered")
        s_scat = sem("rows_added")
        s_added = sem("tile_added")
        s_G = sem("gate_done")
        s_U = sem("up_done")
        s_X = sem("x_transposed")
        s_A = sem("act_transposed")
        s_Y = sem("down_done")
        s_gread = sem("gate_read")
        s_gmin = sem("gate_clipped")
        s_sig = sem("sigmoid_done")
        s_glu = sem("glu_done")
        s_uread = sem("up_read")
        s_uclip = sem("up_clipped")
        s_act = sem("act_ready")
        s_ahi = sem("act_hi")
        s_alo = sem("act_lo")
        s_xTev = sem("xT_evacuated")
        s_aTev = sem("aT_evacuated")
        s_y0 = sem("y_weighted")
        s_y = sem("y_ready")
        block = ctx.enter_context(nc.Block())

        def start_of(eng, e):
            return eng.value_load(tile_start[0:1, at(nc, e, E)], min_val=0, max_val=MAXT - 4)

        def load_bias(sp, e, par):
            for lo, hi, src in ((0, I, g["b_gate"]), (I, 2 * I, g["b_up"]), (2 * I, 2 * I + H, g["b_down"])):
                sp.dma_start(bias[:, par, lo:hi], src[at(nc, e, E - 1), :].to_broadcast([P, hi - lo])).then_inc(s_bias, 16)

        def load_slots(sp, dst, i, done):
            row = sp.value_load(slot_row[0:1, at(nc, i, MAXT - 1)], min_val=0, max_val=slots.shape[0] - P)
            sp.dma_start(dst[:], slots[bass.ds(row, P), :]).then_inc(done, 16)

        @block.sync
        def _(sp):
            load_slots(sp, idxg, 0, s_idxg)
            load_bias(sp, 0, 0)
            sp.wait_ge(s_xg, 16)
            load_slots(sp, idxg, 1, s_idxg)

            def step(i, e, j, more, prev_guard):
                def prev():
                    alone(sp, s_added, i, s_past)
                    load_slots(sp, idxs, i - 1, s_idxs)
                guarded(sp, prev_guard, prev)
                sp.wait_ge(s_xg, 16 * i + 32)
                load_slots(sp, idxg, i + 2, s_idxg)
                if j is not None:
                    def loads():
                        for c in LOAD[j]:
                            alone(sp, s_wlo, NCHUNK * e + NCHUNK + c - RING + 1, s_past)
                            load_chunk(sp, e + 1, c)
                    guarded(sp, more[j], loads)

            with sp.Fori(0, PAIRS) as pair:
                for par in range(2):
                    e = pair * 2 + par
                    t0, t1 = start_of(sp, e), start_of(sp, e + 1)
                    some = pair < PAIRS - 1
                    more = [None if par == 0 else some] * 2 + [some]
                    for j in range(MIN_TILES):
                        step(t0 + j, e, j, more, pair > 0 if par == 0 and j == 0 else None)
                    if par == 0:
                        sp.wait_ge(s_y, t0 + 1)
                        load_bias(sp, e + 1, 1 - par)
                    else:
                        with sp.If(some):
                            sp.wait_ge(s_y, t0 + 1)
                            load_bias(sp, e + 1, 1 - par)
                    with sp.If(t1 > t0 + MIN_TILES):
                        with sp.Fori(t0 + MIN_TILES, t1) as i:
                            step(i, e, None, None, None)
            tt = start_of(sp, E)
            alone(sp, s_added, tt, s_past)
            load_slots(sp, idxs, tt - 1, s_idxs)
            alone(sp, s_idxg, 16 * tt + 32, s_past)

        @block.gpsimd
        def _(pool):
            def gather(i):
                alone(pool, s_idxg, 16 * i + 16, s_past)
                pool.indirect_dma_start(out=xg[:], out_offset=None, in_=xn_tab[:, :],
                                        in_offset=bass.IndirectOffsetOnAxis(idxg[:, 0:1].bitcast(U32), 0)).then_inc(s_xg, 16)

            def scatter(i):
                alone(pool, s_y, i + 1, s_past)
                pool.indirect_dma_start(out=acc[:, :], out_offset=bass.IndirectOffsetOnAxis(idxs[:, 0:1].bitcast(U32), 0),
                                        in_=y[:], in_offset=None, compute_op=ALU.add).then_inc(s_scat, 16)

            pool.sem_inc(s_added, 1)
            tt = start_of(pool, E)
            gather(0)
            pool.wait_ge(s_X, 1)
            gather(1)
            pool.wait_ge(s_X, 2)
            gather(2)
            scatter(0)
            with pool.Fori(2, tt + 1) as i:
                pool.wait_ge(s_X, i + 1)
                gather(i + 1)
                pool.wait_ge(s_scat, 16 * i - 16)
                pool.sem_inc(s_added, 1)
                scatter(i - 1)
            alone(pool, s_xg, 16 * tt + 32, s_past)
            alone(pool, s_scat, 16 * tt, s_past)

        @block.scalar
        def _(act):
            def evac_x(i):
                act.wait_ge(s_X, i + 1)
                act.activation(xT[:].rearrange("p k q a -> p (k q a)").bitcast(F32), psX[:], ACT.Copy).then_inc(s_xTev, 1)

            def evac_a(i):
                act.wait_ge(s_A, i + 1)
                act.activation(aT[:].rearrange("p k q a -> p (k q a)").bitcast(F32), psA[:], ACT.Copy).then_inc(s_aTev, 1)

            def weigh_y(i):
                act.wait_ge(s_idxs, 16 * i + 16)
                act.wait_ge(s_added, i + 1)
                act.wait_ge(s_Y, i + 1)
                act.activation(y[:], psY[:], ACT.Copy, scale=idxs[:, 2:3].bitcast(F32)).then_inc(s_y0, 1)

            act.sem_inc(s_y0, 1)
            evac_x(0)

            def step(i, e, par, t0, j, more, prev_guard):
                def free_gate_up():
                    alone(act, s_U, t0, s_past)

                def cut_one(n):
                    c = CUT[j][n]
                    if c == 0:
                        guarded(act, prev_guard, free_gate_up)
                    if c == 2 * PER_W:
                        act.wait_ge(s_Y, t0 + 1)
                    cut_hi(act, e + 1, 1 - par, c)

                if j is not None:
                    guarded(act, more, lambda: cut_one(0))
                act.wait_ge(s_gmin, i + 1)
                act.activation(sg[:], gt[:], ACT.Sigmoid, scale=ALPHA).then_inc(s_sig, 1)
                guarded(act, prev_guard, lambda: evac_a(i - 1))
                if j is not None:
                    guarded(act, more, lambda: cut_one(1))
                evac_x(i + 1)
                act.wait_ge(s_act, i + 1)
                act.activation(ahl[:, :, HI], av[:], ACT.Copy, scale=S_ACT).then_inc(s_ahi, 1)
                guarded(act, prev_guard, lambda: weigh_y(i - 1))

            with act.Fori(0, PAIRS) as pair:
                for par in range(2):
                    e = pair * 2 + par
                    t0, t1 = start_of(act, e), start_of(act, e + 1)
                    for j in range(MIN_TILES):
                        step(t0 + j, e, par, t0, j, pair < PAIRS - 1 if par else None,
                             pair > 0 if par == 0 and j == 0 else None)
                    with act.If(t1 > t0 + MIN_TILES):
                        with act.Fori(t0 + MIN_TILES, t1) as i:
                            step(i, e, par, t0, None, None, None)
            tt = start_of(act, E)
            evac_a(tt - 1)
            weigh_y(tt - 1)

        @block.vector
        def _(dve):
            def finish_y(i, par):
                dve.wait_ge(s_y0, i + 2)
                dve.scalar_tensor_tensor(out=y[:], in0=bias[:, par, 2 * I:], scalar=idxs[:, 1:2].bitcast(F32), in1=y[:],
                                         op0=ALU.mult, op1=ALU.add).then_inc(s_y, 1)

            def step(i, e, par, j, more, prev_guard):
                if j == 0:
                    dve.wait_ge(s_bias, 48 * e + 48)
                dve.wait_ge(s_G, i + 1)
                dve.scalar_tensor_tensor(out=gt[:], in0=psG[:], scalar=1.0 / (S_ROWS * S_W), in1=bias[:, par, 0:I],
                                         op0=ALU.mult, op1=ALU.add).then_inc(s_gread, 1)
                dve.wait_ge(s_gread, i + 1)
                dve.tensor_scalar(gt[:], gt[:], LIMIT, None, ALU.min).then_inc(s_gmin, 1)
                if j is not None:
                    guarded(dve, more, lambda: cut_lo(dve, e + 1, 1 - par, CUT[j][0]))
                dve.wait_ge(s_sig, i + 1)
                dve.tensor_tensor(gt[:], gt[:], sg[:], ALU.mult).then_inc(s_glu, 1)
                dve.wait_ge(s_U, i + 1)
                dve.scalar_tensor_tensor(out=up[:], in0=psU[:], scalar=1.0 / (S_ROWS * S_W), in1=bias[:, par, I:2 * I],
                                         op0=ALU.mult, op1=ALU.add).then_inc(s_uread, 1)
                dve.wait_ge(s_uread, i + 1)
                dve.tensor_scalar(up[:], up[:], LIMIT, -LIMIT, ALU.min, ALU.max).then_inc(s_uclip, 1)
                dve.wait_ge(s_glu, i + 1)
                dve.wait_ge(s_uclip, i + 1)
                dve.scalar_tensor_tensor(out=av[:], in0=up[:], scalar=1.0, in1=gt[:], op0=ALU.add, op1=ALU.mult).then_inc(s_act, 1)
                if j is not None:
                    guarded(dve, more, lambda: cut_lo(dve, e + 1, 1 - par, CUT[j][1]))
                dve.wait_ge(s_ahi, i + 1)
                dve.scalar_tensor_tensor(out=ahl[:, :, LO], in0=av[:], scalar=S_ACT, in1=ahl[:, :, HI],
                                         op0=ALU.mult, op1=ALU.subtract).then_inc(s_alo, 1)
                guarded(dve, prev_guard, lambda: finish_y(i - 1, 1 - par if j == 0 else par))

            with dve.Fori(0, PAIRS) as pair:
                for par in range(2):
                    e = pair * 2 + par
                    t0, t1 = start_of(dve, e), start_of(dve, e + 1)
                    for j in range(MIN_TILES):
                        step(t0 + j, e, par, j, pair < PAIRS - 1 if par else None, pair > 0 if par == 0 and j == 0 else None)
                    with dve.If(t1 > t0 + MIN_TILES):
                        with dve.Fori(t0 + MIN_TILES, t1) as i:
                            step(i, e, par, None, None, None)
            tt = start_of(dve, E)
            finish_y(tt - 1, 1)

        @block.tensor
        def _(pe):
            def weights(par, part, first, n):
                return W[:, par, part, first:first + n]

            def rows_times(ps, par, offset, done):
                for k in range(KH):
                    for n, (a, c) in enumerate(PASSES):
                        op = pe.matmul(ps[:], xT[:, k, :, a], weights(par, c, offset + k * I, I),
                                       start=k == 0 and n == 0, stop=k == KH - 1 and n == 2)
                op.then_inc(done, 1)

            def transpose_rows():
                for n in range(KH):
                    op = pe.transpose(psX[:, n * P:(n + 1) * P], xg_w[:, n * P:(n + 1) * P], ident[:])
                op.then_inc(s_X, 1)

            def transpose_act(i):
                pe.wait_ge(s_ahi, i + 1)
                pe.wait_ge(s_alo, i + 1)
                for n in range(KI):
                    op = pe.transpose(psA[:, n * P:(n + 1) * P], ahl_w[:, n * P:(n + 1) * P], ident[:])
                op.then_inc(s_A, 1)

            def down(i, par):
                pe.wait_ge(s_aTev, i + 1)
                pe.wait_ge(s_y0, i + 1)
                for h in range(2):
                    for k in range(KI):
                        for n, (a, c) in enumerate(PASSES):
                            op = pe.matmul(psY[:, h * HALF:(h + 1) * HALF], aT[:, k, :, a],
                                           weights(par, c, 2 * KH * I + k * H + h * HALF, HALF),
                                           start=k == 0 and n == 0, stop=k == KI - 1 and n == 2)
                op.then_inc(s_Y, 1)

            def step(i, e, par, first, prev_guard):
                def weights_cut(chunks):
                    if first:
                        alone(pe, s_wlo, NCHUNK * e + chunks, s_past)

                pe.wait_ge(s_xTev, i + 1)
                weights_cut(PER_W)
                guarded(pe, prev_guard, lambda: pe.wait_ge(s_gread, i))
                rows_times(psG, par, 0, s_G)

                def between():
                    transpose_act(i - 1)
                    pe.wait_ge(s_uread, i)
                guarded(pe, prev_guard, between)
                weights_cut(2 * PER_W)
                rows_times(psU, par, KH * I, s_U)
                pe.wait_ge(s_xg, 16 * i + 32)
                transpose_rows()
                guarded(pe, prev_guard, lambda: down(i - 1, 1 - par if first else par))
                weights_cut(3 * PER_W)

            pe.wait_ge(s_xg, 16)
            transpose_rows()
            with pe.Fori(0, PAIRS) as pair:
                for par in range(2):
                    e = pair * 2 + par
                    t0, t1 = start_of(pe, e), start_of(pe, e + 1)
                    step(t0, e, par, True, pair > 0 if par == 0 else None)
                    with pe.Fori(t0 + 1, t1) as i:
                        step(i, e, par, False, None)
            tt = start_of(pe, E)
            transpose_act(tt - 1)
            down(tt - 1, 1)


_INS = ["x", "ctx_1024", "L0_xattn_Wq", "L0_xattn_bq", "L0_xattn_Wk", "L0_xattn_bk", "L0_ffn_gate_w", "L0_ffn_gate_b",
        "L0_ffn_w_gate", "L0_ffn_b_gate", "L0_ffn_w_up", "L0_ffn_b_up", "L0_ffn_w_down", "L0_ffn_b_down"]


def kernel(**inputs):
    import numpy as _np
    import concourse.bacc as _bacc
    from concourse import mybir as _mybir
    from concourse.bass_utils import run_bass_kernel_spmd as _run

    nc = _bacc.Bacc("TRN2", target_bir_lowering=False, num_devices=1)
    arrays, args = {}, []
    for name in _INS:
        a = _np.ascontiguousarray(inputs[name])
        arrays[f"in_{name}"] = a
        args.append(nc.dram_tensor(f"in_{name}", a.shape, _mybir.dt.from_np(a.dtype), kind="ExternalInput").ap())
    b, l, h = inputs["x"].shape
    args.append(nc.dram_tensor("acc", (b * l + P, h), _mybir.dt.float32, kind="ExternalOutput").ap())
    xattn_moe_kernel(nc, *args)
    r = _run(nc, [arrays], core_ids=[0])
    return r.results[0]["acc"][0:b * l].reshape(b, l, h)
```
